# Optimizing a Trainium2 kernel written in Bass

```python
import numpy as np
import jax
import jax.numpy as jnp

def _softmax(x, axis=-1):
    return jax.nn.softmax(x, axis=axis)

def _gelu(x):
    return jax.nn.gelu(x, approximate=True)

def _silu(x):
    return jax.nn.silu(x)

def _sigmoid(x):
    return jax.nn.sigmoid(x)

def _layernorm(x, axis=-1, eps=1e-05):
    m = jnp.mean(x, axis=axis, keepdims=True)
    v = jnp.var(x, axis=axis, keepdims=True)
    return (x - m) / jnp.sqrt(v + eps)

def _scatter_add(tgt, idx, src, axis=0):
    return tgt.at[idx].add(src)

def _segment_sum(src, seg, n):
    return jax.ops.segment_sum(src, seg, n)
kernel_name = 'mk_macaron_d1_jaxref_r8_2dbc9f'

def setup_inputs(seed: int=0):
    np.random.seed(seed)
    _w = jnp.asarray

    def _L0_attn_setup():
        import jax, jax.numpy as jnp
        import numpy as np
        B, S, EMB = (2, 256, 512)
        NHEADS, KVHEADS, HEAD_D = (32, 8, 128)
        SPLITS = (NHEADS * HEAD_D, KVHEADS * HEAD_D, KVHEADS * HEAD_D)
        key = jax.random.key(seed)
        k1, k2, k3 = jax.random.split(key, 3)
        q = jax.random.normal(k1, (B, S, EMB), dtype=jnp.float32)
        w_qkv = jax.random.normal(k2, (sum(SPLITS), EMB), dtype=jnp.float32) * 0.02
        w_dense = jax.random.normal(k3, (EMB, NHEADS * HEAD_D), dtype=jnp.float32) * 0.02
        return {'q': q, 'w_qkv': w_qkv, 'w_dense': w_dense}
    _L0_attn_in = _L0_attn_setup()

    def _L0_ffn_setup():
        import jax, jax.numpy as jnp
        import numpy as np
        HIDDEN = 512
        MOE_INTER = 128
        SHARED_INTER = 512
        NUM_EXPERTS = 16
        TOP_K = 2

        def _moe_forward(x, gate_w, w_gate_up, w_down, shared_w_gate_up, shared_w_down):
            orig_shape = x.shape
            x2 = x.reshape(-1, orig_shape[-1])
            gu_s = x2 @ shared_w_gate_up.T
            g_s, u_s = jnp.split(gu_s, 2, axis=-1)
            shared_out = jax.nn.silu(g_s) * u_s @ shared_w_down.T
            logits = x2 @ gate_w.T
            probs = jax.nn.softmax(logits, axis=-1)
            topk_vals, topk_idx = jax.lax.top_k(probs, TOP_K)
            topk_vals = topk_vals / jnp.sum(topk_vals, axis=-1, keepdims=True)
            combine = jnp.sum(jax.nn.one_hot(topk_idx, NUM_EXPERTS, dtype=x2.dtype) * topk_vals[..., None], axis=1)
            gu = jnp.einsum('th,eih->eti', x2, w_gate_up)
            g, u = jnp.split(gu, 2, axis=-1)
            act = jax.nn.silu(g) * u
            out_e = jnp.einsum('eti,ehi->eth', act, w_down)
            moe_out = jnp.einsum('eth,te->th', out_e, combine)
            return (moe_out + shared_out).reshape(orig_shape)
        key = jax.random.key(seed)
        ks = jax.random.split(key, 6)
        s = 0.02
        hidden_states = jax.random.normal(ks[0], (2, 256, HIDDEN), dtype=jnp.float32)
        gate_w = jax.random.normal(ks[1], (NUM_EXPERTS, HIDDEN), dtype=jnp.float32) * s
        w_gate_up = jax.random.normal(ks[2], (NUM_EXPERTS, 2 * MOE_INTER, HIDDEN), dtype=jnp.float32) * s
        w_down = jax.random.normal(ks[3], (NUM_EXPERTS, HIDDEN, MOE_INTER), dtype=jnp.float32) * s
        shared_w_gate_up = jax.random.normal(ks[4], (2 * SHARED_INTER, HIDDEN), dtype=jnp.float32) * s
        shared_w_down = jax.random.normal(ks[5], (HIDDEN, SHARED_INTER), dtype=jnp.float32) * s
        return {'hidden_states': hidden_states, 'gate_w': gate_w, 'w_gate_up': w_gate_up, 'w_down': w_down, 'shared_w_gate_up': shared_w_gate_up, 'shared_w_down': shared_w_down}
    _L0_ffn_in = _L0_ffn_setup()
    _d = {'L0_attn_q': _L0_attn_in['q'], 'L0_attn_w_qkv': _L0_attn_in['w_qkv'], 'L0_attn_w_dense': _L0_attn_in['w_dense'], 'L0_ffn_gate_w': _L0_ffn_in['gate_w'], 'L0_ffn_w_gate_up': _L0_ffn_in['w_gate_up'], 'L0_ffn_w_down': _L0_ffn_in['w_down'], 'L0_ffn_shared_w_gate_up': _L0_ffn_in['shared_w_gate_up'], 'L0_ffn_shared_w_down': _L0_ffn_in['shared_w_down']}
    _x0 = _d['L0_attn_q']
    _d['L0_attn_q'] = jax.random.normal(jax.random.fold_in(jax.random.key(seed), 1), (2, 512, 512), dtype=_x0.dtype)
    del _x0
    return _d

def reference(L0_attn_q, L0_attn_w_qkv, L0_attn_w_dense, L0_ffn_gate_w, L0_ffn_w_gate_up, L0_ffn_w_down, L0_ffn_shared_w_gate_up, L0_ffn_shared_w_down):

    def _L0_attn_ref(q, w_qkv, w_dense):
        import jax, jax.numpy as jnp
        import numpy as np
        B, S, EMB = (2, 256, 512)
        NHEADS, KVHEADS, HEAD_D = (32, 8, 128)
        SPLITS = (NHEADS * HEAD_D, KVHEADS * HEAD_D, KVHEADS * HEAD_D)
        Bq, Sq, _ = q.shape
        qkv = q @ w_qkv.T
        qs, ks, vs = jnp.split(qkv, np.cumsum(SPLITS)[:-1], axis=-1)
        G = NHEADS // KVHEADS
        qh = qs.reshape(Bq, Sq, KVHEADS, G, HEAD_D)
        kh = ks.reshape(Bq, Sq, KVHEADS, HEAD_D)
        vh = vs.reshape(Bq, Sq, KVHEADS, HEAD_D)
        scale = 1.0 / jnp.sqrt(jnp.float32(HEAD_D))
        scores = jnp.einsum('bskgd,btkd->bkgst', qh, kh) * scale
        causal = jnp.tril(jnp.ones((Sq, Sq), dtype=bool))
        scores = jnp.where(causal, scores, jnp.finfo(scores.dtype).min)
        probs = jax.nn.softmax(scores, axis=-1)
        attn = jnp.einsum('bkgst,btkd->bskgd', probs, vh)
        attn = attn.reshape(Bq, Sq, NHEADS * HEAD_D)
        return attn @ w_dense.T

    def _L0_ffn_ref(hidden_states, gate_w, w_gate_up, w_down, shared_w_gate_up, shared_w_down):
        import jax, jax.numpy as jnp
        import numpy as np
        HIDDEN = 512
        MOE_INTER = 128
        SHARED_INTER = 512
        NUM_EXPERTS = 16
        TOP_K = 2

        def _moe_forward(x, gate_w, w_gate_up, w_down, shared_w_gate_up, shared_w_down):
            orig_shape = x.shape
            x2 = x.reshape(-1, orig_shape[-1])
            gu_s = x2 @ shared_w_gate_up.T
            g_s, u_s = jnp.split(gu_s, 2, axis=-1)
            shared_out = jax.nn.silu(g_s) * u_s @ shared_w_down.T
            logits = x2 @ gate_w.T
            probs = jax.nn.softmax(logits, axis=-1)
            topk_vals, topk_idx = jax.lax.top_k(probs, TOP_K)
            topk_vals = topk_vals / jnp.sum(topk_vals, axis=-1, keepdims=True)
            combine = jnp.sum(jax.nn.one_hot(topk_idx, NUM_EXPERTS, dtype=x2.dtype) * topk_vals[..., None], axis=1)
            gu = jnp.einsum('th,eih->eti', x2, w_gate_up)
            g, u = jnp.split(gu, 2, axis=-1)
            act = jax.nn.silu(g) * u
            out_e = jnp.einsum('eti,ehi->eth', act, w_down)
            moe_out = jnp.einsum('eth,te->th', out_e, combine)
            return (moe_out + shared_out).reshape(orig_shape)
        return _moe_forward(hidden_states, gate_w, w_gate_up, w_down, shared_w_gate_up, shared_w_down)
    x = L0_attn_q
    x = x + 0.5 * _L0_ffn_ref(_layernorm(x, axis=-1), L0_ffn_gate_w, L0_ffn_w_gate_up, L0_ffn_w_down, L0_ffn_shared_w_gate_up, L0_ffn_shared_w_down)
    x = x + _L0_attn_ref(_layernorm(x, axis=-1), L0_attn_w_qkv, L0_attn_w_dense)
    x = x + 0.5 * _L0_ffn_ref(_layernorm(x, axis=-1), L0_ffn_gate_w, L0_ffn_w_gate_up, L0_ffn_w_down, L0_ffn_shared_w_gate_up, L0_ffn_shared_w_down)
    return x

_drawn_inputs = setup_inputs


def setup_inputs(seed=0):
    import zlib

    import numpy as np

    out = dict(_drawn_inputs(seed))
    spreads = {}
    factors = {'L0_ffn_gate_w': 3.481, 'L0_ffn_w_gate_up': 3.236, 'L0_ffn_w_down': 3.238}
    for name, (base, spread) in spreads.items():
        noise = np.random.default_rng([zlib.crc32(name.encode()), seed]).standard_normal(out[name].shape)
        drawn = base * np.exp(spread * noise) if base else spread * noise
        out[name] = jnp.asarray(drawn.astype(out[name].dtype))
    for name, factor in factors.items():
        out[name] = (out[name] * factor).astype(out[name].dtype)
    return out
```

```python
from contextlib import ExitStack
from collections import namedtuple

import concourse.bass as bass
from concourse import mybir

F32 = mybir.dt.float32
F32R = mybir.dt.float32r
U32 = mybir.dt.uint32
I32 = mybir.dt.int32
ALU = mybir.AluOpType
ACT = mybir.ActivationFunctionType
AX_X = mybir.AxisListType.X

P = 128
BATCH, SEQ, HID = 2, 512, 512
TOK = BATCH * SEQ
TT = TOK // P
HC = HID // P
NEXP, INTER = 16, 128
NSH = 4
NALL = NEXP + NSH
GU = HC * 2 * INTER
FW = GU + HID
KV, G, D = 8, 4, 128
ST = SEQ // P
SCORE_SCALE = float(D) ** -0.5
MASKED = -1.0e30
EPS = 1e-5
TRI = [P * i * (i + 1) // 2 for i in range(ST + 1)]
COL = [0, 512, 896, 1152]
PARTS = ((0, 0), (0, 1), (1, 0))


def build(nc, x_in, ffn_w, gate_w, wq, wkv, wd, out):
    keep = ExitStack()
    with keep:
        def sb(name, shape, dt, stack=keep):
            return stack.enter_context(nc.sbuf_tensor(name, shape, dt))

        def pair(name, shape, stack=keep):
            return [sb(f"{name}_hi", shape, F32R, stack), sb(f"{name}_lo", shape, F32R, stack)]

        def sem(name):
            return keep.enter_context(nc.semaphore(name))

        def sems(prefix, names):
            return namedtuple("Sems", names)(*[sem(f"{prefix}_{n}") for n in names.split()])

        bank = [keep.enter_context(nc.psum_tensor(f"bank{i}", [P, 512], F32)) for i in range(8)]

        x = sb("x", [P, TT, HID], F32)
        xnT = pair("xnT", [P, HC, TOK])
        ident = sb("ident", [P, P], F32)
        causal = sb("causal", [P, 512], F32)
        raw_q = sb("raw_q", [P, G, HC, D], F32)
        raw_kv = sb("raw_kv", [P, 2, HC, D], F32)
        raw_d = sb("raw_d", [P, G, HID], F32)
        gw_raw = sb("gw_raw", [P, HC, NEXP], F32)
        gw = pair("gw", [P, HC, NEXP])
        eid_i = sb("eid_i", [P, NEXP], I32)
        eid = sb("eid", [P, NEXP], F32)
        stats = sb("stats", [P, TT, 6], F32)
        mv = sb("mv", [P, TT, 2], F32)
        idle = sb("idle", [P, ST], F32)
        rvar = sb("rvar", [P, TT], F32)
        veps = sb("veps", [P, TT], F32)
        root = sb("root", [P, TT], F32)
        newt = sb("newt", [P, TT], F32)
        rstd = sb("rstd", [P, TT], F32)

        with ExitStack() as st:
            xn = sb("xn", [P, TT, HID], F32, st)
            raw_w = [sb(f"raw_w{p}", [P, FW], F32, st) for p in range(2)]
            wgu = [pair(f"wgu{p}", [P, HC, 2, INTER], st) for p in range(2)]
            wdn = [pair(f"wdn{p}", [P, HID], st) for p in range(2)]
            sg = [sb(f"sg{p}", [P, 512], F32, st) for p in range(2)]
            hb = [sb(f"hb{p}", [P, 512], F32, st) for p in range(2)]
            ab = [pair(f"ab{p}", [P, 512], st) for p in range(2)]
            lmax = sb("lmax", [P, TT], F32, st)
            lsub = sb("lsub", [P, TT, NEXP], F32, st)
            lexp = sb("lexp", [P, TT, NEXP], F32, st)
            lsum = sb("lsum", [P, TT], F32, st)
            lrec = sb("lrec", [P, TT], F32, st)
            prob = sb("prob", [P, TT, NEXP], F32, st)
            top8 = sb("top8", [P, TT, 8], F32, st)
            idx8 = sb("idx8", [P, TT, 8], U32, st)
            idxf = sb("idxf", [P, TT, 8], F32, st)
            tsum = sb("tsum", [P, TT], F32, st)
            trec = sb("trec", [P, TT], F32, st)
            wtop = sb("wtop", [P, TT, 2], F32, st)
            hot = [sb(f"hot{n}", [P, TT, NEXP], F32, st) for n in range(2)]
            comb = sb("comb", [P, NALL, TT], F32, st)

        with ExitStack() as st:
            wqs = [pair(f"wqs{r}", [P, HC, D], st) for r in range(G)]
            wks = pair("wks", [P, HC, D], st)
            wvs = pair("wvs", [P, HC, D], st)
            wds = [pair(f"wds{r}", [P, HID], st) for r in range(G)]
            qT = pair("qT", [P, SEQ], st)
            kT = [pair(f"kT{b}", [P, SEQ], st) for b in range(2)]
            vT = sb("vT", [P, SEQ], F32, st)
            vv = [pair(f"vv{b}", [P, ST, D], st) for b in range(2)]
            sp_ = [sb(f"scores{p}", [P, TRI[ST]], F32, st) for p in range(2)]
            pT = pair("pT", [P, TRI[ST]], st)
            oT = [[pair(f"oT{b}_{r}", [P, SEQ], st) for r in range(G)] for b in range(2)]
            nmax = [sb(f"nmax{p}", [P, ST], F32, st) for p in range(2)]
            psumr = [sb(f"psumr{p}", [P, ST], F32, st) for p in range(2)]
            pinv = [sb(f"pinv{p}", [P, ST], F32, st) for p in range(2)]

        loaded = sems("loaded", "x gate q kv d")
        consts = sems("consts", "mem sel causal eid")
        NORMS = 3
        norm = [sems(f"norm{n}", "chain var root mul transposed hi lo") for n in range(NORMS)]
        route = [sems(f"route{n}", "gate_hi gate_lo logits sub exp chain ready") for n in range(2)]
        ffn = [sems(f"ffn{n}", "loaded0 loaded1 gu_hi gu_lo dn_hi dn_lo g_mm u_mm silu mul act_hi act_lo d_mm added")
               for n in range(2)]
        att = sems("att", "w_hi w_lo proj_mm proj_hi proj_out s_mm masked exp inv normed t_mm t_hi t_lo "
                          "pv_mm pv_hi pv_lo o_mm added")
        stored = sem("stored")

        def wait(eng, s, value):
            if isinstance(value, int) and value <= 0:
                return
            eng.wait_ge(s, value)

        block = keep.enter_context(nc.Block())

        def ffn_slots(eng, slot):
            for k in range(4):
                slot(0, k)
            with eng.Fori(1, NALL // 2 - 1) as it:
                for k in range(4):
                    slot(it, k)
            for k in range(5):
                slot(NALL // 2 - 1, k)

        def exists(s, first, last):
            return first <= s <= last if isinstance(s, int) else True

        def att_slots(eng, slot):
            for k in range(8):
                slot(0, k)
            with eng.Fori(1, KV - 1) as g:
                for k in range(8):
                    slot(g, k)
            for k in range(8 + 5):
                slot(KV - 1, k)

        UNITS = KV * BATCH * G
        PROJ_AHEAD = 4
        QPOS = (0, 1, 3, 5)

        def qpos(u, r, among=QPOS):
            return r if isinstance(u, int) and u >= UNITS - G else among[r]

        XPOS = (None, 2, 4, 6)

        def first_cuts(cut):
            flat = "p c d -> p (c d)"
            for n, (w, raw) in enumerate([(wks, raw_kv[:, 0]), (wvs, raw_kv[:, 1])]
                                         + [(wqs[r], raw_q[:, r]) for r in range(G)]):
                cut(w[0][:].rearrange(flat), w[1][:].rearrange(flat), raw.rearrange(flat), n + 1)

        def cuts(g, k, cut):
            flat = "p c d -> p (c d)"
            base = 6 + 10 * g
            if k == 4:
                for r in range(G):
                    n = base + 3 + r if exists(8 * g + k, 0, UNITS - 9) else base + 1 + r
                    cut(wds[r][0][:], wds[r][1][:], raw_d[:, r], n)
            if exists(8 * g + k, 0, UNITS - 9):
                if k == 3:
                    cut(wks[0][:].rearrange(flat), wks[1][:].rearrange(flat), raw_kv[:, 0].rearrange(flat), base + 1)
                    cut(wvs[0][:].rearrange(flat), wvs[1][:].rearrange(flat), raw_kv[:, 1].rearrange(flat), base + 2)
                if 4 <= k <= 7:
                    r = k - 4
                    cut(wqs[r][0][:].rearrange(flat), wqs[r][1][:].rearrange(flat), raw_q[:, r].rearrange(flat),
                        base + 7 + r)

        @block.sync
        def _(sp):
            xv = x_in.rearrange("(t p) h -> p t h", p=P)
            for half in range(2):
                sp.dma_start(x[:, 4 * half:4 * half + 4, :], xv[:, 4 * half:4 * half + 4, :]).then_inc(loaded.x, 16)
                sp.wait_ge(loaded.x, 16 * (half + 1))
            sp.dma_start(gw_raw[:], gate_w).then_inc(loaded.gate, 16)

            def load_pieces(n):
                f = ffn[n]
                ld = (f.loaded0, f.loaded1)
                for e in range(2):
                    sp.dma_start(raw_w[e][:], ffn_w[e]).then_inc(ld[e], 16)
                with sp.Fori(1, NALL // 2) as it:
                    for p in range(2):
                        sp.wait_ge(f.dn_hi, 2 * it - 1 + p)
                        sp.wait_ge(f.dn_lo, 2 * it - 1 + p)
                        sp.dma_start(raw_w[p][:], ffn_w[bass.ds(2 * it + p, 1), :, :].rearrange("a p n -> (a p) n")
                                     ).then_inc(ld[p], 16)

            load_pieces(0)
            sp.dma_start(raw_kv[:], wkv[0]).then_inc(loaded.kv, 16)
            sp.dma_start(raw_q[:], wq[0]).then_inc(loaded.q, 16)
            sp.dma_start(raw_d[:], wd[0]).then_inc(loaded.d, 16)
            with sp.Fori(1, KV) as g:
                wait(sp, att.w_hi, 6 + 10 * (g - 1))
                wait(sp, att.w_lo, 6 + 10 * (g - 1))
                sp.dma_start(raw_kv[:], wkv[bass.ds(g, 1)].rearrange("a p k c d -> (a p) k c d")).then_inc(loaded.kv, 16)
                sp.dma_start(raw_q[:], wq[bass.ds(g, 1)].rearrange("a p r c d -> (a p) r c d")).then_inc(loaded.q, 16)
                wait(sp, att.w_hi, 6 + 10 * (g - 1) + 6)
                wait(sp, att.w_lo, 6 + 10 * (g - 1) + 6)
                sp.dma_start(raw_d[:], wd[bass.ds(g, 1)].rearrange("a p r h -> (a p) r h")).then_inc(loaded.d, 16)
            sp.wait_ge(att.added, UNITS)
            load_pieces(1)
            sp.wait_ge(ffn[1].added, 4 * 2 * NALL)
            sp.dma_start(out.rearrange("(t p) h -> p t h", p=P), x[:]).then_inc(stored, 16)
            sp.wait_ge(stored, 16)

        @block.gpsimd
        def _(pool):
            nc.gpsimd.memset(ident[:], 0.0).then_inc(consts.mem, 1)
            nc.gpsimd.memset(causal[:], 0.0).then_inc(consts.mem, 1)
            nc.gpsimd.iota(eid_i[:], pattern=[[1, NEXP]], base=0, channel_multiplier=0).then_inc(consts.mem, 1)
            pool.wait_ge(consts.mem, 3)
            nc.gpsimd.affine_select(out=ident[:], in_=ident[:], compare_op=ALU.not_equal, fill=1.0, base=0,
                                    pattern=[[-1, P]], channel_multiplier=1).then_inc(consts.sel, 1)
            nc.gpsimd.affine_select(out=causal[:, 384:512], in_=causal[:, 384:512], compare_op=ALU.is_ge, fill=MASKED,
                                    base=0, pattern=[[-1, P]], channel_multiplier=1).then_inc(consts.causal, 1)
            nc.gpsimd.tensor_copy(eid[:], eid_i[:]).then_inc(consts.eid, 1)

            def cut_ffn(n):
                f, ld = ffn[n], (ffn[n].loaded0, ffn[n].loaded1)

                def low_gu(it, p):
                    pool.wait_ge(ld[p], 16 * (it + 1))
                    pool.wait_ge(f.gu_hi, 2 * it + p + 1)
                    nc.gpsimd.tensor_tensor(wgu[p][1][:].rearrange("p c k i -> p (c k i)"), raw_w[p][:, 0:GU],
                                            wgu[p][0][:].bitcast(F32).rearrange("p c k i -> p (c k i)"),
                                            ALU.subtract).then_inc(f.gu_lo, 1)

                def low_dn(it, p):
                    pool.wait_ge(f.dn_hi, 2 * it + p + 1)
                    nc.gpsimd.tensor_tensor(wdn[p][1][:], raw_w[p][:, GU:FW], wdn[p][0][:].bitcast(F32),
                                            ALU.subtract).then_inc(f.dn_lo, 1)

                for p in range(2):
                    low_gu(0, p)
                    low_dn(0, p)
                with pool.Fori(1, NALL // 2) as it:
                    for p in range(2):
                        low_gu(it, p)
                        low_dn(it, p)

            def slot(g, k):
                u = 8 * g + k
                r = k % 4
                if exists(u, 0, UNITS - 1):
                    for i in (3, 2, 0, 1):
                        if i == 3:
                            wait(pool, att.inv, u + 1)
                        s = sp_[k % 2][:, TRI[i]:TRI[i + 1]]
                        nc.gpsimd.tensor_tensor(s, s, pinv[k % 2][:, i:i + 1].to_broadcast([P, P * (i + 1)]),
                                                ALU.mult).then_inc(att.normed, 1)
                cuts(g, k, low_part)

            def low_part(hi, lo, raw, count):
                wait(pool, att.w_hi, count)
                nc.gpsimd.tensor_tensor(lo, raw, hi.bitcast(F32), ALU.subtract).then_inc(att.w_lo, 1)

            cut_ffn(0)
            first_cuts(low_part)
            att_slots(pool, slot)
            cut_ffn(1)

        @block.scalar
        def _(act):
            def layer_norm(n):
                act.wait_ge(norm[n].var, 1)
                nc.scalar.activation(root[:], rvar[:], ACT.Sqrt).then_inc(norm[n].root, 1)
                for t in range(TT):
                    act.wait_ge(norm[n].transposed, t + 1)
                    nc.scalar.activation(xnT[0][:, :, t * P:(t + 1) * P],
                                         bank[t % 4][:].rearrange("p (c t) -> p c t", c=HC),
                                         ACT.Copy).then_inc(norm[n].hi, 1)

            def router(n):
                if n == 0:
                    act.wait_ge(loaded.gate, 16)
                    nc.scalar.activation(gw[0][:], gw_raw[:], ACT.Copy).then_inc(route[n].gate_hi, 1)
                act.wait_ge(route[n].sub, 1)
                nc.scalar.activation(lexp[:], lsub[:], ACT.Exp).then_inc(route[n].exp, 1)

            def feed_forward(n):
                f, ld = ffn[n], (ffn[n].loaded0, ffn[n].loaded1)

                def cut_gu(it, p):
                    act.wait_ge(ld[p], 16 * (it + 1))
                    wait(act, f.u_mm, 4 * it + 2 * p - 2)
                    nc.scalar.activation(wgu[p][0][:].rearrange("p c k i -> p (c k i)"), raw_w[p][:, 0:GU],
                                         ACT.Copy).then_inc(f.gu_hi, 1)

                def cut_dn(it, p):
                    wait(act, f.d_mm, 4 * (4 * it + 2 * p - 2))
                    nc.scalar.activation(wdn[p][0][:], raw_w[p][:, GU:FW], ACT.Copy).then_inc(f.dn_hi, 1)

                def slot(it, k):
                    s, par = 4 * it + k, k % 2
                    if exists(s, 0, 2 * NALL - 1):
                        act.wait_ge(f.g_mm, s + 1)
                        wait(act, f.mul, s - 1)
                        nc.scalar.activation(sg[par][:], bank[par][:], ACT.Silu).then_inc(f.silu, 1)
                        act.wait_ge(f.mul, s + 1)
                        wait(act, f.d_mm, 4 * (s - 1))
                        nc.scalar.activation(ab[par][0][:], hb[par][:], ACT.Copy).then_inc(f.act_hi, 1)
                    if k == 0 and exists(s, 2, 2 * NALL - 2):
                        cut_gu(it, 1)
                    if k == 1:
                        if exists(s, 2, 2 * NALL - 2):
                            cut_dn(it, 1)
                    if k == 2 and exists(s, 0, 2 * NALL - 3):
                        cut_gu(it + 1, 0)
                    if k == 3 and exists(s, 0, 2 * NALL - 3):
                        cut_dn(it + 1, 0)

                for p in range(2):
                    cut_gu(0, p)
                    cut_dn(0, p)
                ffn_slots(act, slot)

            def attention():
                def high_part(hi, lo, raw, count):
                    nc.scalar.activation(hi, raw, ACT.Copy).then_inc(att.w_hi, 1)

                def high_parts(g, k):
                    u = 8 * g + k
                    if k == 3 and exists(u, 0, UNITS - 9):
                        act.wait_ge(loaded.kv, 16 * (g + 2))
                        act.wait_ge(att.proj_mm, PROJ_AHEAD + 7 * (2 * g) + XPOS[2] + 1)
                    if 4 <= k <= 7 and exists(u, 0, UNITS - 9):
                        act.wait_ge(loaded.q, 16 * (g + 2))
                        act.wait_ge(att.proj_mm, PROJ_AHEAD + 7 * (2 * g + (k - 1) // 4) + QPOS[(k - 1) % 4] + 1)
                    if k == 4:
                        act.wait_ge(loaded.d, 16 * (g + 1))
                        wait(act, att.o_mm, u - 4)
                    cuts(g, k, high_part)

                def turned_hi(u, n, lo_col, hi_col, b):
                    act.wait_ge(att.t_mm, 3 * u + n + 1)
                    if n == 0:
                        wait(act, att.pv_mm, u)
                    nc.scalar.activation(pT[0][:, lo_col:hi_col], bank[b][:, 0:hi_col - lo_col],
                                         ACT.Copy).then_inc(att.t_hi, 1)

                def slot(g, k):
                    u, par, r, b = 8 * g + k, k % 2, k % 4, (k // 4) % 2
                    quad = 2 * g + k // 4
                    if exists(u, 1, UNITS):
                        turned_hi(u - 1, 0, COL[0], COL[1], 6)
                        turned_hi(u - 1, 1, COL[1], COL[2], 7)
                    if exists(u, 0, UNITS - 1):
                        for n, i in enumerate((3, 2, 0, 1)):
                            act.wait_ge(att.masked, 4 * u + n + 1)
                            s = sp_[par][:, TRI[i]:TRI[i + 1]]
                            nc.scalar.activation(s, s, ACT.Exp, bias=nmax[par][:, i:i + 1], scale=-1.0,
                                                 accum_out=psumr[par][:, i:i + 1]).then_inc(att.exp, 1)
                    if exists(u, 1, UNITS):
                        turned_hi(u - 1, 2, COL[2], TRI[ST], 6)
                    if exists(u, 0, UNITS - 2):
                        act.wait_ge(att.proj_mm, PROJ_AHEAD + 7 * quad + qpos(u, r) + 1)
                        nc.scalar.activation(qT[0][:], bank[0][:], ACT.Copy).then_inc(att.proj_hi, 1)
                    if exists(u, 1, UNITS):
                        ru, bu = (k - 1) % 4, ((k - 1) // 4) % 2
                        act.wait_ge(att.pv_mm, u)
                        wait(act, att.o_mm, u - 1 - ru - 4)
                        nc.scalar.activation(oT[bu][ru][0][:], bank[1][:], ACT.Copy).then_inc(att.pv_hi, 1)
                    if r in (1, 3) and exists(u, 0, UNITS - 5):
                        act.wait_ge(att.proj_mm, PROJ_AHEAD + 7 * quad + XPOS[r] + 1)
                        if r == 1:
                            nc.scalar.activation(kT[1 - b][0][:], bank[0][:], ACT.Copy).then_inc(att.proj_hi, 1)
                        else:
                            nc.scalar.activation(vv[1 - b][0][:].rearrange("p c d -> p (c d)"), bank[0][:],
                                                 ACT.Copy).then_inc(att.proj_hi, 1)
                    if k < 8:
                        high_parts(g, k)

                act.wait_ge(norm[1].lo, TT)
                act.wait_ge(loaded.kv, 16)
                act.wait_ge(loaded.q, 16)
                first_cuts(high_part)
                for n, dst in ((1, kT[0][0][:]), (3, vv[0][0][:].rearrange("p c d -> p (c d)")), (4, qT[0][:])):
                    act.wait_ge(att.proj_mm, n)
                    nc.scalar.activation(dst, bank[0][:], ACT.Copy).then_inc(att.proj_hi, 1)
                att_slots(act, slot)

            layer_norm(0)
            router(0)
            feed_forward(0)
            layer_norm(1)
            attention()
            layer_norm(2)
            router(1)
            feed_forward(1)

        @block.vector
        def _(dve):
            def layer_norm(n):
                s = norm[n]
                for t in range(TT):
                    if n == 0:
                        if t % 4 == 0:
                            dve.wait_ge(loaded.x, 16 * (t // 4 + 1))
                    if n == 1 and t == 0:
                        dve.wait_ge(ffn[0].added, 8 * NALL)
                    if n == 2 and t == 0:
                        dve.wait_ge(att.added, UNITS)
                    nc.vector.bn_stats(stats[:, t, :], x[:, t, :]).then_inc(s.chain, 1)
                for t in range(TT):
                    dve.wait_ge(s.chain, t + 1)
                    nc.vector.bn_aggr(mv[:, t, :], stats[:, t, :]).then_inc(s.chain, 1)
                dve.wait_ge(s.chain, 2 * TT)
                nc.vector.tensor_scalar(veps[:], mv[:, :, 1], EPS, None, ALU.add).then_inc(s.chain, 1)
                dve.wait_ge(s.chain, 2 * TT + 1)
                nc.vector.reciprocal(rvar[:], veps[:]).then_inc(s.var, 1)
                dve.wait_ge(s.root, 1)
                nc.vector.tensor_tensor(newt[:], root[:], root[:], ALU.mult).then_inc(s.chain, 1)
                dve.wait_ge(s.chain, 2 * TT + 2)
                nc.vector.tensor_tensor(newt[:], newt[:], veps[:], ALU.mult).then_inc(s.chain, 1)
                dve.wait_ge(s.chain, 2 * TT + 3)
                nc.vector.tensor_scalar(newt[:], newt[:], -0.5, 1.5, ALU.mult, ALU.add).then_inc(s.chain, 1)
                dve.wait_ge(s.chain, 2 * TT + 4)
                nc.vector.tensor_tensor(rstd[:], newt[:], root[:], ALU.mult).then_inc(s.chain, 1)
                dve.wait_ge(s.chain, 2 * TT + 5)
                for t in range(TT):
                    nc.vector.tensor_scalar(xn[:, t, :], x[:, t, :], mv[:, t, 0:1], rstd[:, t:t + 1], ALU.subtract,
                                            ALU.mult).then_inc(s.mul, 1)
                for t in range(TT):
                    dve.wait_ge(s.hi, t + 1)
                    nc.vector.tensor_tensor(xnT[1][:, :, t * P:(t + 1) * P],
                                            bank[t % 4][:].rearrange("p (c t) -> p c t", c=HC),
                                            xnT[0][:, :, t * P:(t + 1) * P].bitcast(F32),
                                            ALU.subtract).then_inc(s.lo, 1)

            def router(n):
                s = route[n]
                count = [0]

                def then(ins):
                    count[0] += 1
                    ins.then_inc(s.chain, 1)
                    dve.wait_ge(s.chain, count[0])

                if n == 0:
                    dve.wait_ge(s.gate_hi, 1)
                    nc.vector.tensor_tensor(gw[1][:], gw_raw[:], gw[0][:].bitcast(F32),
                                            ALU.subtract).then_inc(s.gate_lo, 1)
                logits = bank[4][:, 0:TT * NEXP].rearrange("p (t e) -> p t e", e=NEXP)
                dve.wait_ge(s.logits, 1)
                then(nc.vector.tensor_reduce(lmax[:], logits, AX_X, ALU.max))
                nc.vector.tensor_tensor(lsub[:], logits, lmax[:].unsqueeze(2).to_broadcast([P, TT, NEXP]),
                                        ALU.subtract).then_inc(s.sub, 1)
                dve.wait_ge(s.exp, 1)
                then(nc.vector.tensor_reduce(lsum[:], lexp[:], AX_X, ALU.add))
                then(nc.vector.reciprocal(lrec[:], lsum[:]))
                then(nc.vector.tensor_tensor(prob[:], lexp[:], lrec[:].unsqueeze(2).to_broadcast([P, TT, NEXP]),
                                             ALU.mult))
                for t in range(TT):
                    last = nc.vector.max(top8[:, t, :], prob[:, t, :])
                then(last)
                for t in range(TT):
                    last = nc.vector.max_index(idx8[:, t, :], top8[:, t, :], prob[:, t, :])
                then(last)
                then(nc.vector.tensor_copy(idxf[:], idx8[:]))
                then(nc.vector.tensor_tensor(tsum[:], top8[:, :, 0], top8[:, :, 1], ALU.add))
                then(nc.vector.reciprocal(trec[:], tsum[:]))
                then(nc.vector.tensor_scalar(trec[:], trec[:], 0.5, None, ALU.mult))
                then(nc.vector.tensor_tensor(wtop[:], top8[:, :, 0:2], trec[:].unsqueeze(2).to_broadcast([P, TT, 2]),
                                             ALU.mult))
                dve.wait_ge(consts.eid, 1)
                for m in range(2):
                    then(nc.vector.tensor_tensor(hot[m][:], eid[:].unsqueeze(1).to_broadcast([P, TT, NEXP]),
                                                 idxf[:, :, m:m + 1].to_broadcast([P, TT, NEXP]), ALU.is_equal))
                    then(nc.vector.tensor_tensor(hot[m][:], hot[m][:],
                                                 wtop[:, :, m:m + 1].to_broadcast([P, TT, NEXP]), ALU.mult))
                then(nc.vector.tensor_tensor(comb[:, 0:NEXP, :].rearrange("p e t -> p t e"), hot[0][:], hot[1][:],
                                             ALU.add))
                then(nc.vector.memset(comb[:, NEXP:NALL, :], 0.5))

            def feed_forward(n):
                f = ffn[n]
                combf = comb[:].rearrange("p e t -> p (e t)")

                def slot(it, k):
                    s, par = 4 * it + k, k % 2
                    if exists(s, 0, 2 * NALL - 1):
                        dve.wait_ge(f.silu, s + 1)
                        dve.wait_ge(f.u_mm, s + 1)
                        nc.vector.tensor_tensor(hb[par][:], sg[par][:], bank[2 + par][:], ALU.mult).then_inc(f.mul, 1)
                    if exists(s, 1, 2 * NALL):
                        pk = (k - 1) % 4
                        e = 2 * it + (k - 1) // 2
                        for t in range(4):
                            tile = 4 * (pk % 2) + t
                            dve.wait_ge(f.d_mm, 4 * (s - 1) + t + 1)
                            wait(dve, f.added, 4 * (s - 3) + t + 1)
                            nc.vector.scalar_tensor_tensor(out=x[:, tile, :], in0=bank[4 + t][:],
                                                           scalar=combf[:, bass.ds(e * TT + tile, 1)],
                                                           in1=x[:, tile, :], op0=ALU.mult,
                                                           op1=ALU.add).then_inc(f.added, 1)
                    if exists(s, 0, 2 * NALL - 1):
                        dve.wait_ge(f.act_hi, s + 1)
                        nc.vector.tensor_tensor(ab[par][1][:], hb[par][:], ab[par][0][:].bitcast(F32),
                                                ALU.subtract).then_inc(f.act_lo, 1)

                ffn_slots(dve, slot)

            def attention():
                def turned_lo(u, n, lo_col, hi_col, b):
                    dve.wait_ge(att.t_hi, 3 * u + n + 1)
                    nc.vector.tensor_tensor(pT[1][:, lo_col:hi_col], bank[b][:, 0:hi_col - lo_col],
                                            pT[0][:, lo_col:hi_col].bitcast(F32), ALU.subtract).then_inc(att.t_lo, 1)

                def low(dst, src, hi, s):
                    nc.vector.tensor_tensor(dst, src, hi.bitcast(F32), ALU.subtract).then_inc(s, 1)

                def slot(g, k):
                    u, par, r, b = 8 * g + k, k % 2, k % 4, (k // 4) % 2
                    quad = 2 * g + k // 4
                    if exists(u, 0, UNITS - 1):
                        for n, (i, bk, c) in enumerate(((3, 3, 0), (2, 4, 0), (0, 4, 384), (1, 5, 0))):
                            if n != 2:
                                dve.wait_ge(att.s_mm, 3 * u + (0, 1, 1, 2)[n] + 1)
                                nc.vector.memset(idle[:, n:n + 1], 0.0)
                            w = P * (i + 1)
                            nc.vector.tensor_tensor_reduce(sp_[par][:, TRI[i]:TRI[i + 1]], bank[bk][:, c:c + w],
                                                           causal[:, 512 - w:512], -SCORE_SCALE, 3.0e38, ALU.add,
                                                           ALU.min, nmax[par][:, i:i + 1]).then_inc(att.masked, 1)
                    if exists(u, 1, UNITS):
                        turned_lo(u - 1, 0, COL[0], COL[1], 6)
                        turned_lo(u - 1, 1, COL[1], COL[2], 7)
                    if exists(u, 0, UNITS - 1):
                        dve.wait_ge(att.exp, 4 * u + 4)
                        nc.vector.reciprocal(pinv[par][:], psumr[par][:]).then_inc(att.inv, 1)
                    if exists(u, 1, UNITS):
                        turned_lo(u - 1, 2, COL[2], TRI[ST], 6)
                    if exists(u, 0, UNITS - 2):
                        dve.wait_ge(att.proj_hi, 3 + 6 * quad + qpos(u, r, (0, 1, 3, 4)) + 1)
                        low(qT[1][:], bank[0][:], qT[0][:], att.proj_out)
                    if exists(u, 5, UNITS + 4):
                        tile = (3, 4, 5, 6, 7, 0, 1, 2)[k % 8]
                        dve.wait_ge(att.o_mm, u - 4)
                        nc.vector.tensor_tensor(x[:, tile, :], bank[2][:], x[:, tile, :], ALU.add).then_inc(att.added, 1)
                    if exists(u, 1, UNITS):
                        ru, bu = (k - 1) % 4, ((k - 1) // 4) % 2
                        dve.wait_ge(att.pv_hi, u)
                        low(oT[bu][ru][1][:], bank[1][:], oT[bu][ru][0][:], att.pv_lo)
                    if exists(u, 0, UNITS - 5):
                        if r == 1:
                            dve.wait_ge(att.proj_hi, 3 + 6 * quad + 2 + 1)
                            low(kT[1 - b][1][:], bank[0][:], kT[1 - b][0][:], att.proj_out)
                        if r == 2:
                            dve.wait_ge(att.proj_mm, PROJ_AHEAD + 7 * quad + XPOS[2] + 1)
                            nc.vector.tensor_copy(vT[:], bank[0][:]).then_inc(att.proj_out, 1)
                        if r == 3:
                            dve.wait_ge(att.proj_hi, 3 + 6 * quad + 5 + 1)
                            low(vv[1 - b][1][:].rearrange("p c d -> p (c d)"), bank[0][:],
                                vv[1 - b][0][:].rearrange("p c d -> p (c d)"), att.proj_out)

                dve.wait_ge(consts.causal, 1)
                dve.wait_ge(att.proj_hi, 1)
                low(kT[0][1][:], bank[0][:], kT[0][0][:], att.proj_out)
                dve.wait_ge(att.proj_mm, 2)
                nc.vector.tensor_copy(vT[:], bank[0][:]).then_inc(att.proj_out, 1)
                dve.wait_ge(att.proj_hi, 2)
                low(vv[0][1][:].rearrange("p c d -> p (c d)"), bank[0][:],
                    vv[0][0][:].rearrange("p c d -> p (c d)"), att.proj_out)
                dve.wait_ge(att.proj_hi, 3)
                low(qT[1][:], bank[0][:], qT[0][:], att.proj_out)
                att_slots(dve, slot)

            layer_norm(0)
            router(0)
            feed_forward(0)
            layer_norm(1)
            attention()
            layer_norm(2)
            router(1)
            feed_forward(1)

        @block.tensor
        def _(pe):
            def layer_norm(n):
                if n == 0:
                    pe.wait_ge(consts.sel, 1)
                for t in range(TT):
                    pe.wait_ge(norm[n].mul, t + 1)
                    if t >= 4:
                        pe.wait_ge(norm[n].lo, t - 3)
                    for c in range(HC):
                        last = nc.tensor.transpose(bank[t % 4][:, c * P:(c + 1) * P], xn[:, t, c * P:(c + 1) * P],
                                                   ident[:])
                    last.then_inc(norm[n].transposed, 1)

            def router(n):
                if n == 0:
                    pe.wait_ge(route[n].gate_lo, 1)
                for t in range(TT):
                    pe.wait_ge(norm[2 * n].lo, t + 1)
                    m = 0
                    for c in range(HC):
                        for a, b in PARTS:
                            last = nc.tensor.matmul(bank[4][:, t * NEXP:(t + 1) * NEXP],
                                                    xnT[a][:, c, t * P:(t + 1) * P], gw[b][:, c, :],
                                                    start=(m == 0), stop=(m == 3 * HC - 1))
                            m += 1
                last.then_inc(route[n].logits, 1)
                pe.wait_ge(route[n].sub, 1)

            def feed_forward(n):
                f = ffn[n]

                def slot(it, k):
                    s, p, tb, par = 4 * it + k, k // 2, k % 2, k % 2
                    if exists(s, 0, 2 * NALL - 1):
                        if tb == 0:
                            pe.wait_ge(f.gu_lo, 2 * it + p + 1)
                        wait(pe, f.mul, s - 1)
                        for half, done in ((0, f.g_mm), (1, f.u_mm)):
                            m = 0
                            for c in range(HC):
                                for a, b in PARTS:
                                    last = nc.tensor.matmul(bank[2 * half + par][:], wgu[p][a][:, c, half, :],
                                                            xnT[b][:, c, tb * SEQ:(tb + 1) * SEQ],
                                                            start=(m == 0), stop=(m == 3 * HC - 1))
                                    m += 1
                            last.then_inc(done, 1)
                    if exists(s, 1, 2 * NALL):
                        pp = ((k - 1) % 4) // 2
                        before = (k - 1) % 2
                        pe.wait_ge(f.dn_lo, 2 * it + (k - 1) // 2 + 1)
                        pe.wait_ge(f.act_lo, s)
                        for t in range(4):
                            wait(pe, f.added, 4 * (s - 2) + t + 1)
                            for m, (a, b) in enumerate(PARTS):
                                last = nc.tensor.matmul(bank[4 + t][:], ab[before][a][:, t * P:(t + 1) * P],
                                                        wdn[pp][b][:], start=(m == 0), stop=(m == 2))
                            last.then_inc(f.d_mm, 1)

                ffn_slots(pe, slot)

            def attention():
                def project(w, b, before):
                    wait(pe, att.proj_out, before)
                    m = 0
                    for c in range(HC):
                        for a, z in PARTS:
                            last = nc.tensor.matmul(bank[0][:], w[a][:, c, :], xnT[z][:, c, b * SEQ:(b + 1) * SEQ],
                                                    start=(m == 0), stop=(m == 3 * HC - 1))
                            m += 1
                    last.then_inc(att.proj_mm, 1)

                def turn_value(before):
                    wait(pe, att.proj_out, before)
                    for j in range(ST):
                        last = nc.tensor.transpose(bank[0][:, j * P:(j + 1) * P], vT[:, j * P:(j + 1) * P], ident[:])
                    last.then_inc(att.proj_mm, 1)

                def turn(par, j, b, at):
                    for i in range(j, ST):
                        last = nc.tensor.transpose(bank[b][:, at + (i - j) * P:at + (i - j + 1) * P],
                                                   sp_[par][:, TRI[i] + j * P:TRI[i] + (j + 1) * P], ident[:])
                    return last

                def slot(g, k):
                    u, par, r, b = 8 * g + k, k % 2, k % 4, (k // 4) % 2
                    quad = 2 * g + k // 4
                    before = PROJ_AHEAD + 7 * quad
                    if exists(u, 0, UNITS - 1):
                        pe.wait_ge(att.proj_out, before if r == 0 else before + qpos(u, r - 1) + 1)
                        for n, (bk, tiles) in enumerate(((3, ((3, 0),)), (4, ((2, 0), (0, 384))), (5, ((1, 0),)))):
                            wait(pe, att.masked, 4 * (u - 1) + (1, 3, 4)[n])
                            for i, c in tiles:
                                for m, (a, z) in enumerate(PARTS):
                                    last = nc.tensor.matmul(bank[bk][:, c:c + P * (i + 1)], qT[a][:, i * P:(i + 1) * P],
                                                            kT[b][z][:, 0:P * (i + 1)], start=(m == 0), stop=(m == 2))
                            last.then_inc(att.s_mm, 1)
                    if exists(u, 1, UNITS):
                        pe.wait_ge(att.normed, 4 * u)
                        wait(pe, att.t_lo, 3 * (u - 1))
                        turn(1 - par, 0, 6, 0).then_inc(att.t_mm, 1)
                        turn(1 - par, 1, 7, 0).then_inc(att.t_mm, 1)
                    if exists(u, 0, UNITS - 2):
                        if k == 7:
                            pe.wait_ge(att.w_lo, 6 + 10 * g + 7)
                        elif k < 3:
                            wait(pe, att.w_lo, 6 + 10 * (g - 1) + 8 + k)
                        project(wqs[(k + 1) % 4], ((k + 1) // 4) % 2, before + qpos(u, r))
                    if exists(u, 1, UNITS):
                        pe.wait_ge(att.t_lo, 3 * (u - 1) + 1)
                        turn(1 - par, 2, 6, 0)
                        turn(1 - par, 3, 6, 256).then_inc(att.t_mm, 1)
                    if exists(u, 5, UNITS + 4):
                        ob = (0, 1, 1, 1, 1, 0, 0, 0)[k % 8]
                        tile = (r - 1) % 4
                        if k == 5:
                            pe.wait_ge(att.w_lo, 6 + 10 * g + (6 if exists(u, 0, UNITS - 9) else 4))
                        if r == 1:
                            pe.wait_ge(att.pv_lo, u - 1)
                        wait(pe, att.added, u - 5)
                        m = 0
                        for h in range(G):
                            for a, z in PARTS:
                                last = nc.tensor.matmul(bank[2][:], oT[ob][h][a][:, tile * P:(tile + 1) * P],
                                                        wds[h][z][:], start=(m == 0), stop=(m == 3 * G - 1))
                                m += 1
                        last.then_inc(att.o_mm, 1)
                    if exists(u, 1, UNITS):
                        bu = ((k - 1) // 4) % 2
                        wait(pe, att.pv_lo, u - 1)
                        for j in range(ST):
                            if j != 3:
                                pe.wait_ge(att.t_lo, 3 * (u - 1) + j + 1)
                            for m, (a, z) in enumerate(PARTS):
                                last = nc.tensor.matmul(bank[1][:, j * P:SEQ], vv[bu][a][:, j, :],
                                                        pT[z][:, COL[j]:COL[j] + SEQ - j * P],
                                                        start=(j == 0 and m == 0), stop=(j == ST - 1 and m == 2),
                                                        skip_group_check=True)
                        last.then_inc(att.pv_mm, 1)
                    if r and exists(u, 0, UNITS - 5):
                        at = before + XPOS[r]
                        if r == 1:
                            if k == 5:
                                pe.wait_ge(att.w_lo, 6 + 10 * g + 2)
                            project(wks, 1 - b, at)
                        if r == 2:
                            project(wvs, 1 - b, at)
                        if r == 3:
                            turn_value(at)

                pe.wait_ge(norm[1].lo, TT)
                pe.wait_ge(att.w_lo, 1)
                project(wks, 0, 0)
                pe.wait_ge(att.w_lo, 2)
                project(wvs, 0, 1)
                turn_value(2)
                pe.wait_ge(att.w_lo, 6)
                project(wqs[0], 0, 3)
                att_slots(pe, slot)

            layer_norm(0)
            router(0)
            feed_forward(0)
            layer_norm(1)
            attention()
            layer_norm(2)
            router(1)
            feed_forward(1)


def _layout(np, q, w_qkv, w_dense, gate, w_gate_up, w_down, sh_gate_up, sh_down):
    gu = w_gate_up.reshape(NEXP, 2, INTER, HC, P).transpose(0, 4, 3, 1, 2).reshape(NEXP, P, GU)
    sgu = sh_gate_up.reshape(2, NSH, INTER, HC, P).transpose(1, 4, 3, 0, 2).reshape(NSH, P, GU)
    dn = w_down.transpose(0, 2, 1)
    sdn = sh_down.reshape(HID, NSH, INTER).transpose(1, 2, 0)
    ffn_w = np.concatenate([np.concatenate([gu, dn], 2), np.concatenate([sgu, sdn], 2)], 0)
    gate_w = gate.reshape(NEXP, HC, P).transpose(2, 1, 0)
    nq = KV * G * D
    wq = w_qkv[:nq].reshape(KV, G, D, HC, P).transpose(0, 4, 1, 3, 2)
    wkv = w_qkv[nq:].reshape(2, KV, D, HC, P).transpose(1, 4, 0, 3, 2)
    wd = w_dense.reshape(HID, KV, G, D).transpose(1, 3, 2, 0)
    return dict(x=q.reshape(TOK, HID), ffn_w=ffn_w, gate_w=gate_w, wq=wq, wkv=wkv, wd=wd)


def kernel(**inputs):
    import numpy as np
    import concourse.bacc as bacc
    from concourse.bass_utils import run_bass_kernel_spmd

    a = {n: np.asarray(v) for n, v in inputs.items()}
    laid = _layout(np, a["L0_attn_q"], a["L0_attn_w_qkv"], a["L0_attn_w_dense"], a["L0_ffn_gate_w"],
                   a["L0_ffn_w_gate_up"], a["L0_ffn_w_down"], a["L0_ffn_shared_w_gate_up"], a["L0_ffn_shared_w_down"])
    nc = bacc.Bacc("TRN2", target_bir_lowering=False, num_devices=1)
    arrays, args = {}, []
    for name, v in laid.items():
        arrays[f"in_{name}"] = np.ascontiguousarray(v)
        args.append(nc.dram_tensor(f"in_{name}", v.shape, mybir.dt.from_np(v.dtype), kind="ExternalInput").ap())
    out = nc.dram_tensor("out_x", (TOK, HID), F32, kind="ExternalOutput").ap()
    build(nc, *args, out)
    r = run_bass_kernel_spmd(nc, [arrays], core_ids=[0])
    return r.results[0]["out_x"].reshape(BATCH, SEQ, HID)
```

```python
from contextlib import ExitStack
from collections import namedtuple

import concourse.bass as bass
from concourse import mybir

F32 = mybir.dt.float32
F32R = mybir.dt.float32r
U32 = mybir.dt.uint32
I32 = mybir.dt.int32
ALU = mybir.AluOpType
ACT = mybir.ActivationFunctionType
AX_X = mybir.AxisListType.X

P = 128
BATCH, SEQ, HID = 2, 512, 512
TOK = BATCH * SEQ
TT = TOK // P
HC = HID // P
NEXP, INTER = 16, 128
NSH = 4
HALF = TT // BATCH
SLOTS = NSH * BATCH
BEFORE = 6
TILES = (2 * TOK + NEXP * (P - 1)) // P
WORDS = TILES // 4 + 1
RING = 4
GU = HC * 2 * INTER
FW = GU + HID
KV, G, D = 8, 4, 128
ST = SEQ // P
SCORE_SCALE = float(D) ** -0.5
MASKED = -1.0e30
EPS = 1e-5
TRI = [P * i * (i + 1) // 2 for i in range(ST + 1)]
COL = [0, 512, 896, 1152]
PARTS = ((0, 0), (0, 1), (1, 0))


def build(nc, x_in, ffn_w, gate_w, wq, wkv, wd, out):
    keep = ExitStack()
    with keep:
        def sb(name, shape, dt, stack=keep):
            return stack.enter_context(nc.sbuf_tensor(name, shape, dt))

        def pair(name, shape, stack=keep):
            return [sb(f"{name}_hi", shape, F32R, stack), sb(f"{name}_lo", shape, F32R, stack)]

        def sem(name):
            return keep.enter_context(nc.semaphore(name))

        def sems(prefix, names):
            return namedtuple("Sems", names)(*[sem(f"{prefix}_{n}") for n in names.split()])

        bank = [keep.enter_context(nc.psum_tensor(f"bank{i}", [P, 512], F32)) for i in range(8)]

        x = sb("x", [P, TT, HID], F32)
        xnT = pair("xnT", [P, HC, TOK])
        ident = sb("ident", [P, P], F32)
        gw_raw = sb("gw_raw", [P, HC, NEXP], F32)
        gw = pair("gw", [P, HC, NEXP])
        stats = sb("stats", [P, TT, 6], F32)
        mv = sb("mv", [P, TT, 2], F32)
        idle = sb("idle", [P, ST], F32)
        rvar = sb("rvar", [P, TT], F32)
        veps = sb("veps", [P, TT], F32)
        root = sb("root", [P, TT], F32)
        newt = sb("newt", [P, TT], F32)
        rstd = sb("rstd", [P, TT], F32)
        ones = sb("ones", [P, P], F32)
        below = sb("below", [P, P], F32)
        earlier = sb("earlier", [P, NEXP, NEXP], F32)
        counts_i = sb("counts_i", [P, TILES + 2], I32)
        counts = sb("counts", [P, TILES + 2], F32)
        wtop = sb("wtop", [P, TT, 2], F32)
        rows = sb("rows", [P, TT, 2], U32)
        tile_w = sb("tile_w", [1, WORDS], I32)

        with ExitStack() as st:
            experts = sb("experts", [P, NEXP * FW], F32, st)
            xn = sb("xn", [P, TT, HID], F32, st)
            raw_w = [sb(f"raw_w{p}", [P, FW], F32, st) for p in range(2)]
            wgu = pair("wgu", [P, HC, 2, INTER], st)
            wdn = pair("wdn", [P, HID], st)
            sg = [sb(f"sg{p}", [P, 512], F32, st) for p in range(2)]
            ab = [pair(f"ab{p}", [P, 512], st) for p in range(2)]
            with ExitStack() as sub:
                lmax = sb("lmax", [P, TT], F32, sub)
                lsub = sb("lsub", [P, TT, NEXP], F32, sub)
                lexp = sb("lexp", [P, TT, NEXP], F32, sub)
                lsum = sb("lsum", [P, TT], F32, sub)
                lrec = sb("lrec", [P, TT], F32, sub)
                prob = sb("prob", [P, TT, NEXP], F32, sub)
                top8 = sb("top8", [P, TT, 8], F32, sub)
                idx8 = sb("idx8", [P, TT, 8], U32, sub)
                idxf = sb("idxf", [P, TT, 8], F32, sub)
                tsum = sb("tsum", [P, TT], F32, sub)
                trec = sb("trec", [P, TT], F32, sub)
                hot = sb("hot", [P, 2, TT, NEXP], F32, sub)
                chosen = sb("chosen", [P, TT, NEXP], F32, sub)
                ntile = sb("ntile", [P, NEXP], F32, sub)
                wide = sb("wide", [P, TILES + 2, NEXP], F32, sub)
                ahead = sb("ahead", [P, NEXP], F32, sub)
                upto = sb("upto", [P, NEXP], F32, sub)
                spot = sb("spot", [P, TT, NEXP], F32, sub)
                rowf = sb("rowf", [P, 2, TT], F32, sub)
                tilef = sb("tilef", [1, TILES + 2], F32, sub)
                wordf = sb("wordf", [1, WORDS], F32, sub)
                logT = [wide[:].rearrange("p t e -> p (t e)")[0:NEXP, 0:SEQ], sg[1][0:NEXP, :]]
            with ExitStack() as sub:
                xT = [sb(f"xT{p}", [P, HC, P], F32, sub) for p in range(2)]
                sgt = [sb(f"sgt{p}", [P, INTER], F32, sub) for p in range(2)]
                ht = [sb(f"ht{p}", [P, INTER], F32, sub) for p in range(2)]
                hT = [sb(f"hT{p}", [P, P], F32, sub) for p in range(2)]

        with ExitStack() as st:
            raw_q = sb("raw_q", [P, G, HC, D], F32, st)
            raw_kv = sb("raw_kv", [P, 2, HC, D], F32, st)
            raw_d = sb("raw_d", [P, G, HID], F32, st)
            with ExitStack() as sub:
                yg = sb("yg", [P, TT, 2, HID], F32, sub)
            oT = [[pair(f"oT0_{r}", [P, SEQ], st) for r in range(G)], [None] * G]
            pT = pair("pT", [P, TRI[ST]], st)
            sp_ = [sb(f"scores{p}", [P, TRI[ST]], F32, st) for p in range(2)]
            wqs = [pair(f"wqs{r}", [P, HC, D], st) for r in range(G)]
            wks = pair("wks", [P, HC, D], st)
            wvs = pair("wvs", [P, HC, D], st)
            wds = [pair(f"wds{r}", [P, HID], st) for r in range(G)]
            kT = [pair("kT0", [P, SEQ], st), None]
            qT = pair("qT", [P, SEQ], st)
            kT[1] = pair("kT1", [P, SEQ], st)
            oT[1][0] = pair("oT1_0", [P, SEQ], st)
            vT = sb("vT", [P, SEQ], F32, st)
            vv = [pair(f"vv{b}", [P, ST, D], st) for b in range(2)]
            causal = sb("causal", [P, 512], F32, st)
            oT[1][1:] = [pair(f"oT1_{r}", [P, SEQ], st) for r in range(1, G)]
            nmax = [sb(f"nmax{p}", [P, ST], F32, st) for p in range(2)]
            psumr = [sb(f"psumr{p}", [P, ST], F32, st) for p in range(2)]
            pinv = [sb(f"pinv{p}", [P, ST], F32, st) for p in range(2)]

        x_rows = nc.dram_tensor("x_rows", [TILES * P, HID], F32).ap()
        y_rows = nc.dram_tensor("y_rows", [TILES * P, HID], F32).ap()

        loaded = sems("loaded", "x0 x1 x2 x3 gate q kv d")
        consts = sems("consts", "mem ident below earlier counts zero causal0 causal")
        NORMS = 3
        norm = [sems(f"norm{n}", "chain var root mul transposed hi lo") for n in range(NORMS)]
        route = [sems(f"route{n}", "gate_hi gate_lo logits out turned sub exp chain chosen ranked table rows cleared scattered")
                 for n in range(2)]
        ffn = [sems(f"ffn{n}", "loaded0 loaded1 gu_hi gu_lo dn_hi dn_lo g_mm u_mm silu mul act_hi act_lo d_mm added")
               for n in range(2)]
        moe = [sems(f"moe{n}", "weights x_mm x_out gu_mm silu mul h_mm h_out y_mm y_out added")
               for n in range(2)]
        gathered = [sem(f"gathered{t}") for t in range(TT)]
        tile_in = [sem(f"tile_in{k}") for k in range(RING)]
        tile_out = [sem(f"tile_out{k}") for k in range(RING)]
        att = sems("att", "w_hi w_lo proj_mm proj_hi proj_out s_mm masked exp inv normed t_mm t_hi t_lo "
                          "pv_mm pv_hi pv_lo o_mm added")
        stored = sem("stored")

        def wait(eng, s, value):
            if isinstance(value, int) and value <= 0:
                return
            eng.wait_ge(s, value)

        block = keep.enter_context(nc.Block())

        def norm_bank(n, t):
            if n == 1:
                return t if t < HALF else 2 * (t % 2)
            return 4 + t % 4

        def copies(n, k, count):
            return 16 * (n * len(range(k, TILES, RING)) + count)

        def tile_steps(eng, step):
            for k in range(4):
                step(0, k)
            with eng.Fori(1, TILES // 4) as it:
                for k in range(4):
                    step(it, k)
            for k in range(TILES % 4 + 1):
                step(TILES // 4, k)

        def exists(s, first, last):
            return first <= s <= last if isinstance(s, int) else True

        def att_slots(eng, slot):
            for k in range(8):
                slot(0, k)
            with eng.Fori(1, KV - 1) as g:
                for k in range(8):
                    slot(g, k)
            for k in range(8 + 1):
                slot(KV - 1, k)

        def att_tail(slot):
            for k in range(8 + 1, 8 + 5):
                slot(KV - 1, k)

        def o_bank(u):
            return bank[(0, 1, 3, 2)[u - UNITS - 1] if isinstance(u, int) and u > UNITS else 2]

        UNITS = KV * BATCH * G
        PROJ_AHEAD = 4
        QPOS = (0, 1, 3, 5)

        def qpos(u, r, among=QPOS):
            return r if isinstance(u, int) and u >= UNITS - G else among[r]

        XPOS = (None, 2, 4, 6)

        def first_cuts(cut):
            flat = "p c d -> p (c d)"
            for n, (w, raw) in enumerate([(wks, raw_kv[:, 0]), (wvs, raw_kv[:, 1])]
                                         + [(wqs[r], raw_q[:, r]) for r in range(G)]):
                cut(w[0][:].rearrange(flat), w[1][:].rearrange(flat), raw.rearrange(flat), n + 1)

        def cuts(g, k, cut):
            flat = "p c d -> p (c d)"
            base = 6 + 10 * g
            if k == 4:
                for r in range(G):
                    n = base + 3 + r if exists(8 * g + k, 0, UNITS - 9) else base + 1 + r
                    cut(wds[r][0][:], wds[r][1][:], raw_d[:, r], n)
            if exists(8 * g + k, 0, UNITS - 9):
                if k == 3:
                    cut(wks[0][:].rearrange(flat), wks[1][:].rearrange(flat), raw_kv[:, 0].rearrange(flat), base + 1)
                    cut(wvs[0][:].rearrange(flat), wvs[1][:].rearrange(flat), raw_kv[:, 1].rearrange(flat), base + 2)
                if 4 <= k <= 7:
                    r = k - 4
                    cut(wqs[r][0][:].rearrange(flat), wqs[r][1][:].rearrange(flat), raw_q[:, r].rearrange(flat),
                        base + 7 + r)

        @block.sync
        def _(sp):
            xv = x_in.rearrange("(t p) h -> p t h", p=P)
            for pair_at, s in enumerate((loaded.x0, loaded.x1, loaded.x2, loaded.x3)):
                part = slice(2 * pair_at, 2 * pair_at + 2)
                sp.dma_start(x[:, part, :], xv[:, part, :]).then_inc(s, 16)
            sp.dma_start(gw_raw[:], gate_w).then_inc(loaded.gate, 16)

            def load_shared(n, e):
                f = ffn[n]
                if e >= 2:
                    sp.wait_ge(f.dn_hi, e - 1)
                    sp.wait_ge(f.dn_lo, e - 1)
                sp.dma_start(raw_w[e % 2][:], ffn_w[NEXP + e]).then_inc((f.loaded0, f.loaded1)[e % 2], 16)

            def load_tile(n, it, k):
                j = 4 * it + k
                wait(sp, moe[n].x_mm, j - RING + 1)
                sp.dma_start(xn[:, k, :], x_rows[bass.ds(j * P, P), :]).then_inc(tile_in[k], 16)

            def store_tile(n, it, k):
                j = 4 * it + k
                sp.wait_ge(moe[n].y_out, j + 1)
                sp.dma_start(y_rows[bass.ds(j * P, P), :], xn[:, RING + k, :]).then_inc(tile_out[k], 16)

            def feed_forward(n):
                if n == 1:
                    sp.wait_ge(att.pv_mm, UNITS)
                for e in range(2):
                    load_shared(n, e)
                if n == 1:
                    sp.wait_ge(att.o_mm, UNITS)
                if n == 0:
                    sp.wait_ge(consts.zero, 1)
                    sp.dma_start(x_rows.rearrange("(j p) h -> p j h", p=P),
                                 experts[:, 0:HID].unsqueeze(1).to_broadcast([P, TILES, HID])
                                 ).then_inc(route[n].cleared, 16)
                    sp.wait_ge(route[n].cleared, 16)
                for e in range(NEXP):
                    if e in (4, 12):
                        load_shared(n, 2 + e // 12)
                    sp.dma_start(experts[:, e * FW:(e + 1) * FW], ffn_w[e]).then_inc(moe[n].weights, 16)
                sp.wait_ge(route[n].scattered, 2 * TT * 16)
                for k in range(4):
                    load_tile(n, 0, k)
                with sp.Fori(1, TILES // 4) as it:
                    for k in range(4):
                        store_tile(n, it - 1, k)
                        load_tile(n, it, k)
                last = TILES // 4
                for k in range(4):
                    store_tile(n, last - 1, k)
                    if k < TILES % 4:
                        load_tile(n, last, k)
                for k in range(TILES % 4):
                    store_tile(n, last, k)

            feed_forward(0)
            sp.wait_ge(moe[0].y_mm, TILES)
            sp.dma_start(raw_kv[:], wkv[0]).then_inc(loaded.kv, 16)
            sp.dma_start(raw_q[:], wq[0]).then_inc(loaded.q, 16)
            sp.dma_start(raw_d[:], wd[0]).then_inc(loaded.d, 16)
            with sp.Fori(1, KV) as g:
                wait(sp, att.w_hi, 6 + 10 * (g - 1))
                wait(sp, att.w_lo, 6 + 10 * (g - 1))
                sp.dma_start(raw_kv[:], wkv[bass.ds(g, 1)].rearrange("a p k c d -> (a p) k c d")).then_inc(loaded.kv, 16)
                sp.dma_start(raw_q[:], wq[bass.ds(g, 1)].rearrange("a p r c d -> (a p) r c d")).then_inc(loaded.q, 16)
                wait(sp, att.w_hi, 6 + 10 * (g - 1) + 6)
                wait(sp, att.w_lo, 6 + 10 * (g - 1) + 6)
                sp.dma_start(raw_d[:], wd[bass.ds(g, 1)].rearrange("a p r h -> (a p) r h")).then_inc(loaded.d, 16)
            feed_forward(1)
            for t in range(TT):
                sp.wait_ge(moe[1].added, 4 * (t // 2) + 3 + t % 2)
                sp.dma_start(out[t * P:(t + 1) * P, :], x[:, t, :]).then_inc(stored, 16)
            sp.wait_ge(stored, TT * 16)

        @block.gpsimd
        def _(pool):
            nc.gpsimd.memset(experts[:, 0:HID], 0.0).then_inc(consts.zero, 1)
            nc.gpsimd.memset(ident[:], 0.0).then_inc(consts.mem, 1)
            nc.gpsimd.memset(ones[:], 1.0).then_inc(consts.mem, 1)
            nc.gpsimd.memset(below[:], 1.0).then_inc(consts.mem, 1)
            nc.gpsimd.memset(earlier[:], 1.0).then_inc(consts.mem, 1)
            nc.gpsimd.iota(counts_i[:], pattern=[[1, TILES + 2]], base=0, channel_multiplier=0).then_inc(consts.mem, 1)
            pool.wait_ge(consts.mem, 5)
            nc.gpsimd.affine_select(out=ident[:], in_=ident[:], compare_op=ALU.not_equal, fill=1.0, base=0,
                                    pattern=[[-1, P]], channel_multiplier=1).then_inc(consts.ident, 1)
            nc.gpsimd.affine_select(out=below[:], in_=below[:], compare_op=ALU.is_gt, fill=0.0, base=0,
                                    pattern=[[1, P]], channel_multiplier=-1).then_inc(consts.below, 1)
            nc.gpsimd.affine_select(out=earlier[:], in_=earlier[:], compare_op=ALU.is_gt, fill=0.0, base=0,
                                    pattern=[[1, NEXP], [-1, NEXP]], channel_multiplier=0).then_inc(consts.earlier, 1)
            nc.gpsimd.tensor_copy(counts[:], counts_i[:]).then_inc(consts.counts, 1)

            def feed_forward(n):
                pool.wait_ge(route[n].rows, 1)
                if n == 0:
                    pool.wait_ge(route[n].cleared, 16)
                for t in range(TT):
                    for m in range(2):
                        nc.gpsimd.indirect_dma_start(
                            out=x_rows, out_offset=bass.IndirectOffsetOnAxis(ap=rows[:, t, m:m + 1], axis=0),
                            in_=xn[:, t, :], in_offset=None).then_inc(route[n].scattered, 16)
                for k in range(RING):
                    pool.wait_ge(tile_out[k], copies(n + 1, k, 0))
                pool.wait_ge(moe[n].y_mm, TILES)
                for t in range(TT):
                    for m in range(2):
                        nc.gpsimd.indirect_dma_start(
                            out=yg[:, t, m, :], out_offset=None, in_=y_rows,
                            in_offset=bass.IndirectOffsetOnAxis(ap=rows[:, t, m:m + 1], axis=0)
                        ).then_inc(gathered[t], 16)

            def slot(g, k):
                u = 8 * g + k
                r = k % 4
                if exists(u, 0, UNITS - 1):
                    for i in (3, 2, 0, 1):
                        if i == 3:
                            wait(pool, att.inv, u + 1)
                        s = sp_[k % 2][:, TRI[i]:TRI[i + 1]]
                        nc.gpsimd.tensor_tensor(s, s, pinv[k % 2][:, i:i + 1].to_broadcast([P, P * (i + 1)]),
                                                ALU.mult).then_inc(att.normed, 1)
                cuts(g, k, low_part)

            def low_part(hi, lo, raw, count):
                wait(pool, att.w_hi, count)
                nc.gpsimd.tensor_tensor(lo, raw, hi.bitcast(F32), ALU.subtract).then_inc(att.w_lo, 1)

            feed_forward(0)
            pool.wait_ge(moe[0].y_mm, TILES)
            first_cuts(low_part)
            pool.wait_ge(ffn[0].dn_hi, NSH)
            pool.wait_ge(ffn[0].dn_lo, NSH)
            nc.gpsimd.memset(causal[:], 0.0).then_inc(consts.causal0, 1)
            pool.wait_ge(consts.causal0, 1)
            nc.gpsimd.affine_select(out=causal[:, 384:512], in_=causal[:, 384:512], compare_op=ALU.is_ge, fill=MASKED,
                                    base=0, pattern=[[-1, P]], channel_multiplier=1).then_inc(consts.causal, 1)
            att_slots(pool, slot)
            feed_forward(1)

        @block.scalar
        def _(act):
            def roots(n, h):
                act.wait_ge(norm[n].var, h + 1)
                part = slice(HALF * h, HALF * h + HALF)
                nc.scalar.activation(root[:, part], rvar[:, part], ACT.Sqrt).then_inc(norm[n].root, 1)

            def turned_norm(n, h):
                for t in range(HALF * h, HALF * h + HALF):
                    act.wait_ge(norm[n].transposed, t + 1)
                    nc.scalar.activation(xnT[0][:, :, t * P:(t + 1) * P],
                                         bank[norm_bank(n, t)][:].rearrange("p (c t) -> p c t", c=HC),
                                         ACT.Copy).then_inc(norm[n].hi, 1)

            def router(n):
                for b in range(BATCH):
                    act.wait_ge(route[n].logits, b + 1)
                    nc.scalar.activation(logT[b], bank[1 + 2 * b][0:NEXP, :],
                                         ACT.Copy).then_inc(route[n].out, 1)
                act.wait_ge(route[n].sub, 1)
                nc.scalar.activation(lexp[:], lsub[:], ACT.Exp).then_inc(route[n].exp, 1)

            def cut_gu(n, e):
                f = ffn[n]
                act.wait_ge((f.loaded0, f.loaded1)[e % 2], 16 * (e // 2 + 1))
                wait(act, f.u_mm, 2 * e)
                nc.scalar.activation(wgu[0][:].rearrange("p c k i -> p (c k i)"), raw_w[e % 2][:, 0:GU],
                                     ACT.Copy).then_inc(f.gu_hi, 1)

            def cut_dn(n, e):
                f = ffn[n]
                wait(act, f.d_mm, 4 * 2 * e)
                nc.scalar.activation(wdn[0][:], raw_w[e % 2][:, GU:FW], ACT.Copy).then_inc(f.dn_hi, 1)

            def shared(n, first, last):
                f = ffn[n]
                for s in range(first, last):
                    par = s % 2
                    act.wait_ge(f.g_mm, s + 1)
                    wait(act, f.act_lo, s - 1)
                    if s == 1:
                        act.wait_ge(route[n].turned, 1)
                    nc.scalar.activation(sg[par][:], bank[par][:], ACT.Silu).then_inc(f.silu, 1)
                    if s % 2 and s // 2 + 1 < NSH:
                        cut_gu(n, s // 2 + 1)
                    act.wait_ge(f.mul, s + 1)
                    wait(act, f.d_mm, 4 * (s - 1))
                    nc.scalar.activation(ab[par][0][:], sg[par][:], ACT.Copy).then_inc(f.act_hi, 1)
                    if s % 2 == 0 and s:
                        cut_dn(n, s // 2)

            def routed(n):
                m = moe[n]

                def turned(par, count):
                    act.wait_ge(m.x_mm, count)
                    nc.scalar.activation(xT[par][:].rearrange("p c t -> p (c t)"), bank[2 + par][:],
                                         ACT.Copy).then_inc(m.x_out, 1)

                def step(it, k):
                    j, par = 4 * it + k, k % 2
                    if exists(j, 1, TILES):
                        act.wait_ge(m.h_mm, j)
                        nc.scalar.activation(hT[1 - par][:], bank[4 + 1 - par][:, 0:P], ACT.Copy).then_inc(m.h_out, 1)
                    if exists(j, 0, TILES - 1):
                        act.wait_ge(m.gu_mm, j + 1)
                        nc.scalar.activation(sgt[par][:], bank[par][:, 0:INTER], ACT.Silu).then_inc(m.silu, 1)
                    if exists(j, 0, TILES - 2):
                        turned(1 - par, j + 2)

                act.wait_ge(route[n].rows, 1)
                turned(0, 1)
                tile_steps(act, step)

            def attention():
                def high_part(hi, lo, raw, count):
                    nc.scalar.activation(hi, raw, ACT.Copy).then_inc(att.w_hi, 1)

                def high_parts(g, k):
                    u = 8 * g + k
                    if k == 3 and exists(u, 0, UNITS - 9):
                        act.wait_ge(loaded.kv, 16 * (g + 2))
                        act.wait_ge(att.proj_mm, PROJ_AHEAD + 7 * (2 * g) + XPOS[2] + 1)
                    if 4 <= k <= 7 and exists(u, 0, UNITS - 9):
                        act.wait_ge(loaded.q, 16 * (g + 2))
                        act.wait_ge(att.proj_mm, PROJ_AHEAD + 7 * (2 * g + (k - 1) // 4) + QPOS[(k - 1) % 4] + 1)
                    if k == 4:
                        act.wait_ge(loaded.d, 16 * (g + 1))
                        wait(act, att.o_mm, u - 4)
                    cuts(g, k, high_part)

                def turned_hi(u, n, lo_col, hi_col, b):
                    act.wait_ge(att.t_mm, 3 * u + n + 1)
                    if n == 0:
                        wait(act, att.pv_mm, u)
                    nc.scalar.activation(pT[0][:, lo_col:hi_col], bank[b][:, 0:hi_col - lo_col],
                                         ACT.Copy).then_inc(att.t_hi, 1)

                def slot(g, k):
                    u, par, r, b = 8 * g + k, k % 2, k % 4, (k // 4) % 2
                    quad = 2 * g + k // 4
                    if exists(u, 1, UNITS):
                        turned_hi(u - 1, 0, COL[0], COL[1], 6)
                        turned_hi(u - 1, 1, COL[1], COL[2], 7)
                    if exists(u, 0, UNITS - 1):
                        for n, i in enumerate((3, 2, 0, 1)):
                            act.wait_ge(att.masked, 4 * u + n + 1)
                            s = sp_[par][:, TRI[i]:TRI[i + 1]]
                            nc.scalar.activation(s, s, ACT.Exp, bias=nmax[par][:, i:i + 1], scale=-1.0,
                                                 accum_out=psumr[par][:, i:i + 1]).then_inc(att.exp, 1)
                    if exists(u, 1, UNITS):
                        turned_hi(u - 1, 2, COL[2], TRI[ST], 6)
                    if exists(u, 0, UNITS - 2):
                        act.wait_ge(att.proj_mm, PROJ_AHEAD + 7 * quad + qpos(u, r) + 1)
                        nc.scalar.activation(qT[0][:], bank[0][:], ACT.Copy).then_inc(att.proj_hi, 1)
                    if exists(u, 1, UNITS):
                        ru, bu = (k - 1) % 4, ((k - 1) // 4) % 2
                        act.wait_ge(att.pv_mm, u)
                        wait(act, att.o_mm, u - 1 - ru - 4)
                        nc.scalar.activation(oT[bu][ru][0][:], bank[1][:], ACT.Copy).then_inc(att.pv_hi, 1)
                    if isinstance(u, int) and u == 0:
                        roots(1, 1)
                    if isinstance(u, int) and u == 1:
                        turned_norm(1, 1)
                    if r in (1, 3) and exists(u, 0, UNITS - 5):
                        act.wait_ge(att.proj_mm, PROJ_AHEAD + 7 * quad + XPOS[r] + 1)
                        if r == 1:
                            nc.scalar.activation(kT[1 - b][0][:], bank[0][:], ACT.Copy).then_inc(att.proj_hi, 1)
                        else:
                            nc.scalar.activation(vv[1 - b][0][:].rearrange("p c d -> p (c d)"), bank[0][:],
                                                 ACT.Copy).then_inc(att.proj_hi, 1)
                    if k < 8:
                        high_parts(g, k)

                act.wait_ge(loaded.kv, 16)
                act.wait_ge(loaded.q, 16)
                first_cuts(high_part)
                roots(1, 0)
                turned_norm(1, 0)
                for n, dst, b in ((1, kT[0][0][:], 0), (3, qT[0][:], 4),
                                  (4, vv[0][0][:].rearrange("p c d -> p (c d)"), 0)):
                    act.wait_ge(att.proj_mm, n)
                    nc.scalar.activation(dst, bank[b][:], ACT.Copy).then_inc(att.proj_hi, 1)
                att_slots(act, slot)

            def feed_forward(n):
                roots(2 * n, 0)
                if n == 1:
                    act.wait_ge(att.o_mm, UNITS)
                cut_gu(n, 0)
                turned_norm(2 * n, 0)
                roots(2 * n, 1)
                cut_dn(n, 0)
                turned_norm(2 * n, 1)
                if n == 0:
                    act.wait_ge(loaded.gate, 16)
                    nc.scalar.activation(gw[0][:], gw_raw[:], ACT.Copy).then_inc(route[n].gate_hi, 1)
                shared(n, 0, 1)
                router(n)
                shared(n, 1, BEFORE)
                routed(n)
                shared(n, BEFORE, SLOTS)

            feed_forward(0)
            attention()
            feed_forward(1)

        @block.vector
        def _(dve):
            def normalise(n, h):
                s = norm[n]
                part = slice(HALF * h, HALF * h + HALF)
                count = [(2 * HALF + 5) * h]

                def then(ins):
                    count[0] += 1
                    ins.then_inc(s.chain, 1)
                    dve.wait_ge(s.chain, count[0])

                if n == 1:
                    dve.wait_ge(moe[0].added, 2 * HALF * (h + 1))
                if n == 2:
                    dve.wait_ge(att.added, UNITS - HALF * (1 - h))
                for t in range(HALF * h, HALF * h + HALF):
                    if n == 0 and t % 2 == 0:
                        dve.wait_ge((loaded.x0, loaded.x1, loaded.x2, loaded.x3)[t // 2], 16)
                    nc.vector.bn_stats(stats[:, t, :], x[:, t, :]).then_inc(s.chain, 1)
                    count[0] += 1
                for t in range(HALF * h, HALF * h + HALF):
                    dve.wait_ge(s.chain, count[0] - HALF + 1 + t % HALF)
                    nc.vector.bn_aggr(mv[:, t, :], stats[:, t, :]).then_inc(s.chain, 1)
                count[0] += HALF
                dve.wait_ge(s.chain, count[0])
                then(nc.vector.tensor_scalar(veps[:, part], mv[:, part, 1], EPS, None, ALU.add))
                nc.vector.reciprocal(rvar[:, part], veps[:, part]).then_inc(s.var, 1)
                dve.wait_ge(s.root, h + 1)
                then(nc.vector.tensor_tensor(newt[:, part], root[:, part], root[:, part], ALU.mult))
                then(nc.vector.tensor_tensor(newt[:, part], newt[:, part], veps[:, part], ALU.mult))
                then(nc.vector.tensor_scalar(newt[:, part], newt[:, part], -0.5, 1.5, ALU.mult, ALU.add))
                then(nc.vector.tensor_tensor(rstd[:, part], newt[:, part], root[:, part], ALU.mult))
                for t in range(HALF * h, HALF * h + HALF):
                    nc.vector.tensor_scalar(xn[:, t, :], x[:, t, :], mv[:, t, 0:1], rstd[:, t:t + 1], ALU.subtract,
                                            ALU.mult).then_inc(s.mul, 1)

            def turned_norm(n, h):
                s = norm[n]
                for t in range(HALF * h, HALF * h + HALF):
                    dve.wait_ge(s.hi, t + 1)
                    nc.vector.tensor_tensor(xnT[1][:, :, t * P:(t + 1) * P],
                                            bank[norm_bank(n, t)][:].rearrange("p (c t) -> p c t", c=HC),
                                            xnT[0][:, :, t * P:(t + 1) * P].bitcast(F32),
                                            ALU.subtract).then_inc(s.lo, 1)

            def router(n):
                s = route[n]
                count = [0]

                def then(ins):
                    count[0] += 1
                    ins.then_inc(s.chain, 1)
                    dve.wait_ge(s.chain, count[0])

                logits = bank[7][:, 0:TT * NEXP].rearrange("p (t e) -> p t e", e=NEXP)
                dve.wait_ge(s.turned, 1)
                then(nc.vector.tensor_reduce(lmax[:], logits, AX_X, ALU.max))
                nc.vector.tensor_tensor(lsub[:], logits, lmax[:].unsqueeze(2).to_broadcast([P, TT, NEXP]),
                                        ALU.subtract).then_inc(s.sub, 1)
                dve.wait_ge(s.exp, 1)
                then(nc.vector.tensor_reduce(lsum[:], lexp[:], AX_X, ALU.add))
                then(nc.vector.reciprocal(lrec[:], lsum[:]))
                then(nc.vector.tensor_tensor(prob[:], lexp[:], lrec[:].unsqueeze(2).to_broadcast([P, TT, NEXP]),
                                             ALU.mult))
                for t in range(TT):
                    last = nc.vector.max(top8[:, t, :], prob[:, t, :])
                then(last)
                for t in range(TT):
                    last = nc.vector.max_index(idx8[:, t, :], top8[:, t, :], prob[:, t, :])
                then(last)
                then(nc.vector.tensor_copy(idxf[:], idx8[:]))
                then(nc.vector.tensor_tensor(tsum[:], top8[:, :, 0], top8[:, :, 1], ALU.add))
                then(nc.vector.reciprocal(trec[:], tsum[:]))
                then(nc.vector.tensor_scalar(trec[:], trec[:], 0.5, None, ALU.mult))
                then(nc.vector.tensor_tensor(wtop[:], top8[:, :, 0:2], trec[:].unsqueeze(2).to_broadcast([P, TT, 2]),
                                             ALU.mult))
                dve.wait_ge(consts.counts, 1)
                for m in range(2):
                    then(nc.vector.tensor_tensor(hot[:, m], counts[:, 0:NEXP].unsqueeze(1).to_broadcast([P, TT, NEXP]),
                                                 idxf[:, :, m:m + 1].to_broadcast([P, TT, NEXP]), ALU.is_equal))
                nc.vector.tensor_tensor(chosen[:], hot[:, 0], hot[:, 1], ALU.add).then_inc(s.chosen, 1)
                return then

            def place(n, then):
                s = route[n]
                rank = bank[7][:, 0:TT * NEXP].rearrange("p (t e) -> p t e", e=NEXP)
                total = bank[7][:, TT * NEXP:(TT + 1) * NEXP]
                dve.wait_ge(s.ranked, 1)
                then(nc.vector.tensor_scalar(tsum[:], counts[:, 0:TT], float(P), None, ALU.mult))
                then(nc.vector.tensor_tensor(wide[:, 0:TT, :], total.unsqueeze(1).to_broadcast([P, TT, NEXP]),
                                             tsum[:].unsqueeze(2).to_broadcast([P, TT, NEXP]), ALU.is_gt))
                then(nc.vector.tensor_reduce(ntile[:], wide[:, 0:TT, :].rearrange("p t e -> p e t"), AX_X, ALU.add))
                then(nc.vector.tensor_tensor(wide[:, 0:NEXP, :], earlier[:],
                                             ntile[:].unsqueeze(1).to_broadcast([P, NEXP, NEXP]), ALU.mult))
                then(nc.vector.tensor_reduce(ahead[:], wide[:, 0:NEXP, :], AX_X, ALU.add))
                then(nc.vector.tensor_tensor(upto[:], ahead[:], ntile[:], ALU.add))
                then(nc.vector.tensor_scalar(ahead[:], ahead[:], float(P), None, ALU.mult))
                then(nc.vector.tensor_tensor(spot[:], rank, ahead[:].unsqueeze(1).to_broadcast([P, TT, NEXP]), ALU.add))
                then(nc.vector.tensor_tensor(hot[:], hot[:], spot[:].unsqueeze(1).to_broadcast([P, 2, TT, NEXP]),
                                             ALU.mult))
                then(nc.vector.tensor_reduce(rowf[:], hot[:], AX_X, ALU.add))
                then(nc.vector.tensor_copy(rows[:].rearrange("p t m -> p m t"), rowf[:]))
                then(nc.vector.tensor_tensor(wide[0:1], counts[0:1].unsqueeze(2).to_broadcast([1, TILES + 2, NEXP]),
                                             upto[0:1].unsqueeze(1).to_broadcast([1, TILES + 2, NEXP]), ALU.is_gt))
                then(nc.vector.tensor_reduce(tilef[:], wide[0:1], AX_X, ALU.add))
                then(nc.vector.tensor_scalar(tilef[:], tilef[:], float(NEXP - 1), None, ALU.min))
                span = RING * (WORDS - 1) + 1
                then(nc.vector.tensor_copy(wordf[:], tilef[:, 0:span:RING]))
                for m in range(1, RING + 1):
                    then(nc.vector.scalar_tensor_tensor(out=wordf[:], in0=tilef[:, m:m + span:RING],
                                                        scalar=float(NEXP ** m), in1=wordf[:], op0=ALU.mult,
                                                        op1=ALU.add))
                nc.vector.tensor_copy(tile_w[:], wordf[:]).then_inc(s.rows, 1)

            def low_gu(n, e):
                dve.wait_ge(ffn[n].gu_hi, e + 1)
                nc.vector.tensor_tensor(wgu[1][:].rearrange("p c k i -> p (c k i)"), raw_w[e % 2][:, 0:GU],
                                        wgu[0][:].bitcast(F32).rearrange("p c k i -> p (c k i)"),
                                        ALU.subtract).then_inc(ffn[n].gu_lo, 1)

            def low_dn(n, e):
                dve.wait_ge(ffn[n].dn_hi, e + 1)
                nc.vector.tensor_tensor(wdn[1][:], raw_w[e % 2][:, GU:FW], wdn[0][:].bitcast(F32),
                                        ALU.subtract).then_inc(ffn[n].dn_lo, 1)

            def add_down(n, s):
                f = ffn[n]
                for t in range(HALF):
                    tile = HALF * (s % 2) + t
                    dve.wait_ge(f.d_mm, HALF * s + t + 1)
                    wait(dve, f.added, HALF * (s - 2) + t + 1)
                    nc.vector.scalar_tensor_tensor(out=x[:, tile, :], in0=bank[4 + t][:], scalar=0.5,
                                                   in1=x[:, tile, :], op0=ALU.mult, op1=ALU.add).then_inc(f.added, 1)

            def shared(n, first, last):
                f = ffn[n]
                for s in range(first, last):
                    par = s % 2
                    dve.wait_ge(f.silu, s + 1)
                    dve.wait_ge(f.u_mm, s + 1)
                    nc.vector.tensor_tensor(sg[par][:], sg[par][:], bank[2 + par][:], ALU.mult).then_inc(f.mul, 1)
                    if s % 2 and s // 2 + 1 < NSH:
                        low_gu(n, s // 2 + 1)
                    if s and s != BEFORE:
                        add_down(n, s - 1)
                    dve.wait_ge(f.act_hi, s + 1)
                    nc.vector.tensor_tensor(ab[par][1][:], sg[par][:], ab[par][0][:].bitcast(F32),
                                            ALU.subtract).then_inc(f.act_lo, 1)
                    if s % 2 == 0 and s:
                        low_dn(n, s // 2)

            def routed(n):
                m = moe[n]

                def step(it, k):
                    j, par = 4 * it + k, k % 2
                    if exists(j, 0, TILES - 1):
                        dve.wait_ge(m.silu, j + 1)
                        nc.vector.tensor_tensor(ht[par][:], sgt[par][:], bank[par][:, INTER:2 * INTER],
                                                ALU.mult).then_inc(m.mul, 1)
                    if exists(j, 1, TILES):
                        dve.wait_ge(m.y_mm, j)
                        if exists(j, RING + 1, TILES):
                            dve.wait_ge(tile_out[(k - 1) % 4], copies(n, (k - 1) % 4, it + (k - 1) // 4))
                        nc.vector.tensor_copy(xn[:, RING + (k - 1) % 4, :], bank[6 + 1 - par][:]).then_inc(m.y_out, 1)

                dve.wait_ge(route[n].scattered, 2 * TT * 16)
                tile_steps(dve, step)

            def combine(n, h):
                dve.wait_ge(ffn[n].added, HALF * (SLOTS - 1 + h))
                for t in range(HALF * h, HALF * h + HALF, 2):
                    for m in range(2):
                        for tile in (t, t + 1):
                            if m == 0:
                                dve.wait_ge(gathered[tile], 2 * 16 * (n + 1))
                            wait(dve, moe[n].added, 2 * t + 2 * m - 1 + tile - t)
                            nc.vector.scalar_tensor_tensor(out=x[:, tile, :], in0=yg[:, tile, m, :],
                                                           scalar=wtop[:, tile, m:m + 1], in1=x[:, tile, :],
                                                           op0=ALU.mult, op1=ALU.add).then_inc(moe[n].added, 1)

            def attention():
                def turned_lo(u, n, lo_col, hi_col, b):
                    dve.wait_ge(att.t_hi, 3 * u + n + 1)
                    nc.vector.tensor_tensor(pT[1][:, lo_col:hi_col], bank[b][:, 0:hi_col - lo_col],
                                            pT[0][:, lo_col:hi_col].bitcast(F32), ALU.subtract).then_inc(att.t_lo, 1)

                def low(dst, src, hi, s):
                    nc.vector.tensor_tensor(dst, src, hi.bitcast(F32), ALU.subtract).then_inc(s, 1)

                def slot(g, k):
                    u, par, r, b = 8 * g + k, k % 2, k % 4, (k // 4) % 2
                    quad = 2 * g + k // 4
                    if exists(u, 0, UNITS - 1):
                        for n, (i, bk, c) in enumerate(((3, 3, 0), (2, 4, 0), (0, 4, 384), (1, 5, 0))):
                            if n != 2:
                                dve.wait_ge(att.s_mm, 3 * u + (0, 1, 1, 2)[n] + 1)
                                nc.vector.memset(idle[:, n:n + 1], 0.0)
                            w = P * (i + 1)
                            nc.vector.tensor_tensor_reduce(sp_[par][:, TRI[i]:TRI[i + 1]], bank[bk][:, c:c + w],
                                                           causal[:, 512 - w:512], -SCORE_SCALE, 3.0e38, ALU.add,
                                                           ALU.min, nmax[par][:, i:i + 1]).then_inc(att.masked, 1)
                    if exists(u, 1, UNITS):
                        turned_lo(u - 1, 0, COL[0], COL[1], 6)
                        turned_lo(u - 1, 1, COL[1], COL[2], 7)
                    if exists(u, 0, UNITS - 1):
                        dve.wait_ge(att.exp, 4 * u + 4)
                        nc.vector.reciprocal(pinv[par][:], psumr[par][:]).then_inc(att.inv, 1)
                    if exists(u, 1, UNITS):
                        turned_lo(u - 1, 2, COL[2], TRI[ST], 6)
                    if exists(u, 0, UNITS - 2):
                        dve.wait_ge(att.proj_hi, 3 + 6 * quad + qpos(u, r, (0, 1, 3, 4)) + 1)
                        low(qT[1][:], bank[0][:], qT[0][:], att.proj_out)
                    if exists(u, 5, UNITS + 4):
                        tile = (3, 4, 5, 6, 7, 0, 1, 2)[k % 8]
                        dve.wait_ge(att.o_mm, u - 4)
                        nc.vector.tensor_tensor(x[:, tile, :], o_bank(u)[:], x[:, tile, :], ALU.add).then_inc(att.added, 1)
                    if exists(u, 1, UNITS):
                        ru, bu = (k - 1) % 4, ((k - 1) // 4) % 2
                        dve.wait_ge(att.pv_hi, u)
                        low(oT[bu][ru][1][:], bank[1][:], oT[bu][ru][0][:], att.pv_lo)
                    if isinstance(u, int) and u == 0:
                        normalise(1, 1)
                    if isinstance(u, int) and u == 1:
                        turned_norm(1, 1)
                    if exists(u, 0, UNITS - 5):
                        if r == 1:
                            dve.wait_ge(att.proj_hi, 3 + 6 * quad + 2 + 1)
                            low(kT[1 - b][1][:], bank[0][:], kT[1 - b][0][:], att.proj_out)
                        if r == 2:
                            dve.wait_ge(att.proj_mm, PROJ_AHEAD + 7 * quad + XPOS[2] + 1)
                            nc.vector.tensor_copy(vT[:], bank[0][:]).then_inc(att.proj_out, 1)
                        if r == 3:
                            dve.wait_ge(att.proj_hi, 3 + 6 * quad + 5 + 1)
                            low(vv[1 - b][1][:].rearrange("p c d -> p (c d)"), bank[0][:],
                                vv[1 - b][0][:].rearrange("p c d -> p (c d)"), att.proj_out)

                dve.wait_ge(consts.causal, 1)
                dve.wait_ge(att.proj_hi, 1)
                low(kT[0][1][:], bank[0][:], kT[0][0][:], att.proj_out)
                dve.wait_ge(att.proj_mm, 2)
                nc.vector.tensor_copy(vT[:], bank[3][:]).then_inc(att.proj_out, 1)
                dve.wait_ge(att.proj_hi, 2)
                low(qT[1][:], bank[4][:], qT[0][:], att.proj_out)
                dve.wait_ge(att.proj_hi, 3)
                low(vv[0][1][:].rearrange("p c d -> p (c d)"), bank[0][:],
                    vv[0][0][:].rearrange("p c d -> p (c d)"), att.proj_out)
                att_slots(dve, slot)
                normalise(2, 0)
                att_tail(slot)

            def feed_forward(n):
                if n == 0:
                    normalise(2 * n, 0)
                turned_norm(2 * n, 0)
                low_gu(n, 0)
                normalise(2 * n, 1)
                turned_norm(2 * n, 1)
                if n == 0:
                    dve.wait_ge(route[n].gate_hi, 1)
                    nc.vector.tensor_tensor(gw[1][:], gw_raw[:], gw[0][:].bitcast(F32),
                                            ALU.subtract).then_inc(route[n].gate_lo, 1)
                low_dn(n, 0)
                shared(n, 0, 1)
                then = router(n)
                shared(n, 1, 2)
                place(n, then)
                shared(n, 2, BEFORE)
                add_down(n, BEFORE - 1)
                routed(n)
                shared(n, BEFORE, SLOTS)

            feed_forward(0)
            combine(0, 0)
            normalise(1, 0)
            turned_norm(1, 0)
            add_down(0, SLOTS - 1)
            combine(0, 1)
            attention()
            feed_forward(1)
            combine(1, 0)
            add_down(1, SLOTS - 1)
            combine(1, 1)

        @block.tensor
        def _(pe):
            def turn_norm(n, h):
                if n == 0:
                    pe.wait_ge(consts.ident, 1)
                for t in range(HALF * h, HALF * h + HALF):
                    pe.wait_ge(norm[n].mul, t + 1)
                    wait(pe, norm[n].lo, t - 1 if n == 1 and h == 1 else t - 3)
                    for c in range(HC):
                        last = nc.tensor.transpose(bank[norm_bank(n, t)][:, c * P:(c + 1) * P], xn[:, t, c * P:(c + 1) * P],
                                                   ident[:])
                    last.then_inc(norm[n].transposed, 1)

            def router(n):
                if n == 0:
                    pe.wait_ge(route[n].gate_lo, 1)
                for b in range(BATCH):
                    pe.wait_ge(norm[2 * n].lo, HALF * (b + 1))
                    m = 0
                    for c in range(HC):
                        for a, z in PARTS:
                            last = nc.tensor.matmul(bank[1 + 2 * b][0:NEXP, :], gw[a][:, c, :],
                                                    xnT[z][:, c, b * SEQ:(b + 1) * SEQ],
                                                    start=(m == 0), stop=(m == 3 * HC - 1))
                            m += 1
                    last.then_inc(route[n].logits, 1)
                for t in range(TT):
                    if t % HALF == 0:
                        pe.wait_ge(route[n].out, t // HALF + 1)
                    last = nc.tensor.transpose(bank[7][:, t * NEXP:(t + 1) * NEXP], logT[t // HALF][:, t % HALF * P:(t % HALF + 1) * P],
                                               ident[0:NEXP, 0:NEXP])
                last.then_inc(route[n].turned, 1)

            def gate_up(n, s):
                f, tb, par = ffn[n], s % 2, s % 2
                pe.wait_ge(f.gu_lo, s // 2 + 1)
                pe.wait_ge(norm[2 * n].lo, HALF * (tb + 1))
                wait(pe, f.mul, s - 1)
                for half, done in ((0, f.g_mm), (1, f.u_mm)):
                    m = 0
                    for c in range(HC):
                        for a, b in PARTS:
                            last = nc.tensor.matmul(bank[2 * half + par][:], wgu[a][:, c, half, :],
                                                    xnT[b][:, c, tb * SEQ:(tb + 1) * SEQ],
                                                    start=(m == 0), stop=(m == 3 * HC - 1))
                            m += 1
                    last.then_inc(done, 1)

            def down(n, s):
                f = ffn[n]
                pe.wait_ge(f.dn_lo, s // 2 + 1)
                pe.wait_ge(f.act_lo, s + 1)
                for t in range(HALF):
                    wait(pe, f.added, HALF * (s - 1) + t + 1)
                    if s == 0 and t == 3:
                        pe.wait_ge(route[n].sub, 1)
                    if s == 1 and t == 3:
                        pe.wait_ge(route[n].rows, 1)
                    for m, (a, b) in enumerate(PARTS):
                        last = nc.tensor.matmul(bank[4 + t][:], ab[s % 2][a][:, t * P:(t + 1) * P],
                                                wdn[b][:], start=(m == 0), stop=(m == 2))
                    last.then_inc(f.d_mm, 1)

            def rank(n):
                pe.wait_ge(route[n].chosen, 1)
                pe.wait_ge(consts.earlier, 1)
                pe.wait_ge(ffn[n].added, HALF)
                flat = chosen[:].rearrange("p t e -> p (t e)")
                nc.tensor.matmul(bank[7][:, 0:TT * NEXP], below[:], flat, start=True, stop=False,
                                 skip_group_check=True)
                for t in range(TT):
                    last = nc.tensor.matmul(bank[7][:, (t + 1) * NEXP:(TT + 1) * NEXP], ones[:],
                                            chosen[:, t, :].unsqueeze(1).to_broadcast([P, TT - t, NEXP]),
                                            start=False, stop=(t == TT - 1), skip_group_check=True)
                last.then_inc(route[n].ranked, 1)

            def turn(n, k, it, par, count):
                pe.wait_ge(tile_in[k], copies(n, k, it + 1))
                wait(pe, moe[n].x_out, count - 2)
                for c in range(HC):
                    last = nc.tensor.transpose(bank[2 + par][:, c * P:(c + 1) * P], xn[:, k, c * P:(c + 1) * P],
                                               ident[:])
                last.then_inc(moe[n].x_mm, 1)

            def routed(n):
                m = moe[n]

                def steps(it, count):
                    word = pe.value_load(tile_w[0:1, bass.ds(it, 1)], min_val=0, max_val=NEXP ** (RING + 1) - 1)
                    place = {k: (word >> 4 * (k + 1) & NEXP - 1) * FW for k in range(-1, count)}
                    for k in range(count):
                        j, par = 4 * it + k, k % 2
                        if exists(j, 1, TILES):
                            pe.wait_ge(m.mul, j)
                            wait(pe, m.h_out, j - 2)
                            nc.tensor.transpose(bank[4 + 1 - par][:, 0:P], ht[1 - par][:], ident[:]).then_inc(m.h_mm, 1)
                        if exists(j, 0, TILES - 1):
                            pe.wait_ge(m.x_out, j + 1)
                            wait(pe, m.mul, j - 1)
                            for c in range(HC):
                                last = nc.tensor.matmul(bank[par][:, 0:2 * INTER], xT[par][:, c, :],
                                                        experts[:, bass.ds(place[k] + c * 2 * INTER, 2 * INTER)],
                                                        start=(c == 0), stop=(c == HC - 1))
                            last.then_inc(m.gu_mm, 1)
                        if exists(j, 0, TILES - 2):
                            turn(n, (k + 1) % 4, it + (k + 1) // 4, 1 - par, j + 2)
                        if exists(j, 1, TILES):
                            pe.wait_ge(m.h_out, j)
                            wait(pe, m.y_out, j - 2)
                            nc.tensor.matmul(bank[6 + 1 - par][:], hT[1 - par][:],
                                             experts[:, bass.ds(place[k - 1] + GU, HID)],
                                             start=True, stop=True).then_inc(m.y_mm, 1)

                pe.wait_ge(ffn[n].added, HALF * BEFORE)
                pe.wait_ge(route[n].rows, 1)
                pe.wait_ge(moe[n].weights, NEXP * 16)
                steps(0, 4)
                with pe.Fori(1, TILES // 4) as it:
                    steps(it, 4)
                steps(TILES // 4, TILES % 4 + 1)
                pe.wait_ge(m.y_out, TILES)

            def attention():
                def project(w, b, before, into=bank[0]):
                    wait(pe, att.proj_out, before)
                    m = 0
                    for c in range(HC):
                        for a, z in PARTS:
                            last = nc.tensor.matmul(into[:], w[a][:, c, :], xnT[z][:, c, b * SEQ:(b + 1) * SEQ],
                                                    start=(m == 0), stop=(m == 3 * HC - 1))
                            m += 1
                    last.then_inc(att.proj_mm, 1)

                def turn_value(before):
                    wait(pe, att.proj_out, before)
                    for j in range(ST):
                        last = nc.tensor.transpose(bank[0][:, j * P:(j + 1) * P], vT[:, j * P:(j + 1) * P], ident[:])
                    last.then_inc(att.proj_mm, 1)

                def turn(par, j, b, at):
                    for i in range(j, ST):
                        last = nc.tensor.transpose(bank[b][:, at + (i - j) * P:at + (i - j + 1) * P],
                                                   sp_[par][:, TRI[i] + j * P:TRI[i] + (j + 1) * P], ident[:])
                    return last

                def slot(g, k):
                    u, par, r, b = 8 * g + k, k % 2, k % 4, (k // 4) % 2
                    quad = 2 * g + k // 4
                    before = PROJ_AHEAD + 7 * quad
                    if exists(u, 0, UNITS - 1):
                        if isinstance(u, int) and u == 0:
                            pe.wait_ge(att.proj_out, PROJ_AHEAD - 1)
                        else:
                            pe.wait_ge(att.proj_out, before - 1 if r == 0 else before + qpos(u, r - 1) + 1)
                        for n, (bk, tiles) in enumerate(((3, ((3, 0),)), (4, ((2, 0), (0, 384))), (5, ((1, 0),)))):
                            wait(pe, att.masked, 4 * (u - 1) + (1, 3, 4)[n])
                            for i, c in tiles:
                                for m, (a, z) in enumerate(PARTS):
                                    last = nc.tensor.matmul(bank[bk][:, c:c + P * (i + 1)], qT[a][:, i * P:(i + 1) * P],
                                                            kT[b][z][:, 0:P * (i + 1)], start=(m == 0), stop=(m == 2))
                            last.then_inc(att.s_mm, 1)
                    if exists(u, 1, UNITS):
                        pe.wait_ge(att.normed, 4 * u)
                        wait(pe, att.t_lo, 3 * (u - 1))
                        turn(1 - par, 0, 6, 0).then_inc(att.t_mm, 1)
                        turn(1 - par, 1, 7, 0).then_inc(att.t_mm, 1)
                    if exists(u, 0, UNITS - 2):
                        if k == 7:
                            pe.wait_ge(att.w_lo, 6 + 10 * g + 7)
                        elif k < 3:
                            wait(pe, att.w_lo, 6 + 10 * (g - 1) + 8 + k)
                        project(wqs[(k + 1) % 4], ((k + 1) // 4) % 2, before + qpos(u, r))
                    if exists(u, 1, UNITS):
                        pe.wait_ge(att.t_lo, 3 * (u - 1) + 1)
                        turn(1 - par, 2, 6, 0)
                        turn(1 - par, 3, 6, 256).then_inc(att.t_mm, 1)
                    if exists(u, 5, UNITS + 4):
                        ob = (0, 1, 1, 1, 1, 0, 0, 0)[k % 8]
                        tile = (r - 1) % 4
                        if k == 5:
                            pe.wait_ge(att.w_lo, 6 + 10 * g + (6 if exists(u, 0, UNITS - 9) else 4))
                        if r == 1:
                            pe.wait_ge(att.pv_lo, u - 1)
                        wait(pe, att.added, UNITS - HALF if isinstance(u, int) and u > UNITS else u - 5)
                        m = 0
                        for h in range(G):
                            for a, z in PARTS:
                                last = nc.tensor.matmul(o_bank(u)[:], oT[ob][h][a][:, tile * P:(tile + 1) * P],
                                                        wds[h][z][:], start=(m == 0), stop=(m == 3 * G - 1))
                                m += 1
                        last.then_inc(att.o_mm, 1)
                    if exists(u, 1, UNITS):
                        bu = ((k - 1) // 4) % 2
                        wait(pe, att.pv_lo, u - 1)
                        for j in range(ST):
                            if j != 3:
                                pe.wait_ge(att.t_lo, 3 * (u - 1) + j + 1)
                            for m, (a, z) in enumerate(PARTS):
                                last = nc.tensor.matmul(bank[1][:, j * P:SEQ], vv[bu][a][:, j, :],
                                                        pT[z][:, COL[j]:COL[j] + SEQ - j * P],
                                                        start=(j == 0 and m == 0), stop=(j == ST - 1 and m == 2),
                                                        skip_group_check=True)
                        last.then_inc(att.pv_mm, 1)
                    if isinstance(u, int) and u == 1:
                        pe.wait_ge(att.proj_out, before + QPOS[1] + 1)
                        turn_norm(1, 1)
                        pe.wait_ge(norm[1].lo, TT)
                    if r and exists(u, 0, UNITS - 5):
                        at = before + XPOS[r]
                        if r == 1:
                            if k == 5:
                                pe.wait_ge(att.w_lo, 6 + 10 * g + 2)
                            project(wks, 1 - b, at)
                        if r == 2:
                            project(wvs, 1 - b, at)
                        if r == 3:
                            turn_value(at)

                pe.wait_ge(norm[1].lo, HALF)
                pe.wait_ge(att.w_lo, 1)
                project(wks, 0, 0)
                pe.wait_ge(att.w_lo, 2)
                project(wvs, 0, 0, bank[3])
                pe.wait_ge(att.w_lo, 3)
                pe.wait_ge(ffn[0].added, HALF * SLOTS)
                project(wqs[0], 0, 0, bank[4])
                turn_value(2)
                att_slots(pe, slot)
                att_tail(slot)

            def feed_forward(n):
                turn_norm(2 * n, 0)
                gate_up(n, 0)
                turn_norm(2 * n, 1)
                router(n)
                gate_up(n, 1)
                down(n, 0)
                rank(n)
                for s in range(2, BEFORE):
                    gate_up(n, s)
                    down(n, s - 1)
                turn(n, 0, 0, 0, 1)
                down(n, BEFORE - 1)
                routed(n)
                for s in range(BEFORE, SLOTS):
                    gate_up(n, s)
                    if s > BEFORE:
                        down(n, s - 1)
                down(n, SLOTS - 1)

            feed_forward(0)
            turn_norm(1, 0)
            attention()
            feed_forward(1)


def _layout(np, q, w_qkv, w_dense, gate, w_gate_up, w_down, sh_gate_up, sh_down):
    gu = w_gate_up.reshape(NEXP, 2, INTER, HC, P).transpose(0, 4, 3, 1, 2).reshape(NEXP, P, GU)
    sgu = sh_gate_up.reshape(2, NSH, INTER, HC, P).transpose(1, 4, 3, 0, 2).reshape(NSH, P, GU)
    dn = w_down.transpose(0, 2, 1)
    sdn = sh_down.reshape(HID, NSH, INTER).transpose(1, 2, 0)
    ffn_w = np.concatenate([np.concatenate([gu, dn], 2), np.concatenate([sgu, sdn], 2)], 0)
    gate_w = gate.reshape(NEXP, HC, P).transpose(2, 1, 0)
    nq = KV * G * D
    wq = w_qkv[:nq].reshape(KV, G, D, HC, P).transpose(0, 4, 1, 3, 2)
    wkv = w_qkv[nq:].reshape(2, KV, D, HC, P).transpose(1, 4, 0, 3, 2)
    wd = w_dense.reshape(HID, KV, G, D).transpose(1, 3, 2, 0)
    return dict(x=q.reshape(TOK, HID), ffn_w=ffn_w, gate_w=gate_w, wq=wq, wkv=wkv, wd=wd)


def kernel(**inputs):
    import numpy as np
    import concourse.bacc as bacc
    from concourse.bass_utils import run_bass_kernel_spmd

    a = {n: np.asarray(v) for n, v in inputs.items()}
    laid = _layout(np, a["L0_attn_q"], a["L0_attn_w_qkv"], a["L0_attn_w_dense"], a["L0_ffn_gate_w"],
                   a["L0_ffn_w_gate_up"], a["L0_ffn_w_down"], a["L0_ffn_shared_w_gate_up"], a["L0_ffn_shared_w_down"])
    nc = bacc.Bacc("TRN2", target_bir_lowering=False, num_devices=1)
    arrays, args = {}, []
    for name, v in laid.items():
        arrays[f"in_{name}"] = np.ascontiguousarray(v)
        args.append(nc.dram_tensor(f"in_{name}", v.shape, mybir.dt.from_np(v.dtype), kind="ExternalInput").ap())
    out = nc.dram_tensor("out_x", (TOK, HID), F32, kind="ExternalOutput").ap()
    build(nc, *args, out)
    r = run_bass_kernel_spmd(nc, [arrays], core_ids=[0])
    return r.results[0]["out_x"].reshape(BATCH, SEQ, HID)
```

```python
from contextlib import ExitStack
from collections import namedtuple

import concourse.bass as bass
from concourse import mybir

F32 = mybir.dt.float32
F32R = mybir.dt.float32r
U32 = mybir.dt.uint32
I32 = mybir.dt.int32
ALU = mybir.AluOpType
ACT = mybir.ActivationFunctionType
AX_X = mybir.AxisListType.X

P = 128
BATCH, SEQ, HID = 2, 512, 512
TOK = BATCH * SEQ
TT = TOK // P
HC = HID // P
NEXP, INTER = 16, 128
NSH = 4
HALF = TT // BATCH
SLOTS = NSH * BATCH
BEFORE = 6
TILES = (2 * TOK + NEXP * (P - 1)) // P
WORDS = TILES // 4 + 1
LOADED_HALF = NEXP // 2 * 16
EARLY = (1, 8)
RING = 4
GU = HC * 2 * INTER
FRONT = 2 * INTER
FW = GU + HID
KV, G, D = 8, 4, 128
ST = SEQ // P
SCORE_SCALE = float(D) ** -0.5
MASKED = -1.0e30
EPS = 1e-5
TRI = [P * i * (i + 1) // 2 for i in range(ST + 1)]
COL = [0, 512, 896, 1152]
PARTS = ((0, 0), (0, 1), (1, 0))


def build(nc, x_in, ffn_w, gate_w, wq, wkv, wd, out):
    keep = ExitStack()
    with keep:
        def sb(name, shape, dt, stack=keep):
            return stack.enter_context(nc.sbuf_tensor(name, shape, dt))

        def pair(name, shape, stack=keep):
            return [sb(f"{name}_hi", shape, F32R, stack), sb(f"{name}_lo", shape, F32R, stack)]

        def sem(name):
            return keep.enter_context(nc.semaphore(name))

        def sems(prefix, names):
            return namedtuple("Sems", names)(*[sem(f"{prefix}_{n}") for n in names.split()])

        bank = [keep.enter_context(nc.psum_tensor(f"bank{i}", [P, 512], F32)) for i in range(8)]

        x = sb("x", [P, TT, HID], F32)
        xnT = pair("xnT", [P, HC, TOK])
        ident = sb("ident", [P, P], F32)
        gw_raw = sb("gw_raw", [P, HC, NEXP], F32)
        gw = pair("gw", [P, HC, NEXP])
        stats = sb("stats", [P, TT, 6], F32)
        mv = sb("mv", [P, TT, 2], F32)
        idle = sb("idle", [P, ST], F32)
        rvar = sb("rvar", [P, TT], F32)
        veps = sb("veps", [P, TT], F32)
        root = sb("root", [P, TT], F32)
        newt = sb("newt", [P, TT], F32)
        rstd = sb("rstd", [P, TT], F32)
        ones = sb("ones", [P, P], F32)
        below = sb("below", [P, P], F32)
        earlier = sb("earlier", [P, NEXP, NEXP], F32)
        counts_i = sb("counts_i", [P, TILES + 3], I32)
        counts = sb("counts", [P, TILES + 3], F32)
        wtop = sb("wtop", [P, TT, 2], F32)
        rows = sb("rows", [P, TT, 2], U32)
        tile_w = sb("tile_w", [1, WORDS], I32)

        with ExitStack() as st:
            experts = sb("experts", [P, NEXP * FW], F32, st)
            xn = sb("xn", [P, TT, HID], F32, st)
            wgu = pair("wgu", [P, HC, 2, INTER], st)
            wdn = pair("wdn", [P, HID], st)
            with ExitStack() as sub:
                raw_w = [sb(f"raw_w{p}", [P, FW], F32, sub) for p in range(2)]
                sg = [sb(f"sg{p}", [P, 512], F32, sub) for p in range(2)]
                ab = [pair(f"ab{p}", [P, 512], sub) for p in range(2)]
                lmax = sb("lmax", [P, TT], F32, sub)
                lsub = sb("lsub", [P, TT, NEXP], F32, sub)
                lexp = sb("lexp", [P, TT, NEXP], F32, sub)
                lsum = sb("lsum", [P, TT], F32, sub)
                lrec = sb("lrec", [P, TT], F32, sub)
                prob = sb("prob", [P, TT, NEXP], F32, sub)
                top8 = sb("top8", [P, TT, 8], F32, sub)
                idx8 = sb("idx8", [P, TT, 8], U32, sub)
                idxf = sb("idxf", [P, TT, 8], F32, sub)
                tsum = sb("tsum", [P, TT], F32, sub)
                trec = sb("trec", [P, TT], F32, sub)
                hot = sb("hot", [P, 2, TT, NEXP], F32, sub)
                chosen = sb("chosen", [P, TT, NEXP], F32, sub)
                ntile = sb("ntile", [P, NEXP], F32, sub)
                wide = sb("wide", [P, TILES + 3, NEXP], F32, sub)
                ahead = sb("ahead", [P, NEXP], F32, sub)
                upto = sb("upto", [P, NEXP], F32, sub)
                spot = sb("spot", [P, TT, NEXP], F32, sub)
                rowf = sb("rowf", [P, 2, TT], F32, sub)
                tilef = sb("tilef", [1, TILES + 3], F32, sub)
                wordf = sb("wordf", [1, WORDS], F32, sub)
                logT = [wide[:].rearrange("p t e -> p (t e)")[0:NEXP, 0:SEQ], sg[1][0:NEXP, :]]
            with ExitStack() as sub:
                xT = [pair("xT0", [P, HC, P], sub)]
                tfront = pair("tfront", [P, FRONT], sub)
                tdn = [pair(f"tdn{p}", [P, HID], sub) for p in range(2)]
                tback = [None, pair("tback1", [P, GU - FRONT], sub)]
                xT.append(pair("xT1", [P, HC, P], sub))
                tback[0] = pair("tback0", [P, GU - FRONT], sub)
                hT = pair("hT", [P, P], sub)
                ht = sb("ht", [P, INTER], F32, sub)

        with ExitStack() as st:
            raw_q = sb("raw_q", [P, G, HC, D], F32, st)
            raw_kv = sb("raw_kv", [P, 2, HC, D], F32, st)
            raw_d = sb("raw_d", [P, G, HID], F32, st)
            with ExitStack() as sub:
                yg = sb("yg", [P, TT, 2, HID], F32, sub)
            oT = [[pair(f"oT0_{r}", [P, SEQ], st) for r in range(G)], [None] * G]
            pT = pair("pT", [P, TRI[ST]], st)
            sp_ = [sb(f"scores{p}", [P, TRI[ST]], F32, st) for p in range(2)]
            wqs = [pair(f"wqs{r}", [P, HC, D], st) for r in range(G)]
            wks = pair("wks", [P, HC, D], st)
            wvs = pair("wvs", [P, HC, D], st)
            wds = [pair(f"wds{r}", [P, HID], st) for r in range(G)]
            kT = [pair("kT0", [P, SEQ], st), None]
            qT = pair("qT", [P, SEQ], st)
            kT[1] = pair("kT1", [P, SEQ], st)
            oT[1][0] = pair("oT1_0", [P, SEQ], st)
            oT[1][1:] = [pair(f"oT1_{r}", [P, SEQ], st) for r in range(1, G)]
            vT = sb("vT", [P, SEQ], F32, st)
            vv = [pair(f"vv{b}", [P, ST, D], st) for b in range(2)]
            causal = sb("causal", [P, 512], F32, st)
            nmax = [sb(f"nmax{p}", [P, ST], F32, st) for p in range(2)]
            psumr = [sb(f"psumr{p}", [P, ST], F32, st) for p in range(2)]
            pinv = [sb(f"pinv{p}", [P, ST], F32, st) for p in range(2)]

        x_rows = nc.dram_tensor("x_rows", [TILES * P, HID], F32).ap()
        y_rows = nc.dram_tensor("y_rows", [TILES * P, HID], F32).ap()

        loaded = sems("loaded", "x0 x1 x2 x3 gate q kv d")
        consts = sems("consts", "mem ident below earlier counts zero causal0 causal")
        NORMS = 3
        norm = [sems(f"norm{n}", "var root mul transposed hi lo") for n in range(NORMS)]
        norm_chain = sem("norm_chain")
        raw_loaded = [sem(f"raw_loaded{p}") for p in range(2)]
        route = [sems(f"route{n}", "gate_hi gate_lo logits out turned sub exp chain chosen ranked table rows cleared scattered")
                 for n in range(2)]
        ffn = [sems(f"ffn{n}", "gu_hi gu_lo dn_hi dn_lo g_mm u_mm silu mul act_hi act_lo d_mm added")
               for n in range(2)]
        moe = [sems(f"moe{n}", "weights x_mm x_out gu_mm silu mul h_mm h_out y_mm y_out added")
               for n in range(2)]
        tile_part = sems("tile_part", "front_hi front_lo front_mm back_hi middle_lo back_lo dn_hi dn_lo x_lo h_lo")
        gathered = [sem(f"gathered{t}") for t in range(TT)]
        tile_in = [sem(f"tile_in{k}") for k in range(RING)]
        tile_out = [sem(f"tile_out{k}") for k in range(RING)]
        att = sems("att", "w_hi w_lo proj_mm proj_hi proj_out s_mm masked exp inv normed t_mm t_hi t_lo "
                          "pv_mm pv_hi pv_lo o_mm added")
        stored = sem("stored")

        def wait(eng, s, value):
            if isinstance(value, int) and value <= 0:
                return
            eng.wait_ge(s, value)

        block = keep.enter_context(nc.Block())

        def norm_bank(n, t):
            if n == 1:
                return t if t < HALF else 2 * (t % 2)
            return 4 + t % 4

        def copies(n, k, count):
            return 16 * (n * len(range(k, TILES, RING)) + count)

        def places(eng, it, loads=False):
            word = eng.value_load(tile_w[0:1, bass.ds(it, 1)], min_val=0, max_val=NEXP ** (RING + 1) - 1)
            at = [(word >> 4 * k & NEXP - 1) * FW for k in range(RING + 1)]
            if not loads:
                return at, None
            return at, [((word >> 4 * k + 3 & 1) + 1) * LOADED_HALF for k in range(RING + 1)]

        def tile_steps(eng, step, loads=False):
            at, there = places(eng, 0, loads)
            for k in range(4):
                step(0, k, at, there)
            with eng.Fori(1, TILES // 4) as it:
                at, there = places(eng, it, loads)
                for k in range(4):
                    step(it, k, at, there)
            at, there = places(eng, TILES // 4, loads)
            for k in range(TILES % 4 + 1):
                step(TILES // 4, k, at, there)

        def exists(s, first, last):
            return first <= s <= last if isinstance(s, int) else True

        def att_slots(eng, slot):
            for k in range(8):
                slot(0, k)
            with eng.Fori(1, KV - 1) as g:
                for k in range(8):
                    slot(g, k)
            for k in range(8 + 1):
                slot(KV - 1, k)

        def att_tail(slot):
            for k in range(8 + 1, 8 + 5):
                slot(KV - 1, k)

        def o_bank(u):
            return bank[(0, 1, 3, 2)[u - UNITS - 1] if isinstance(u, int) and u > UNITS else 2]

        UNITS = KV * BATCH * G
        PROJ_AHEAD = 4
        QPOS = (0, 1, 3, 5)

        def qpos(u, r, among=QPOS):
            return r if isinstance(u, int) and u >= UNITS - G else among[r]

        XPOS = (None, 2, 4, 6)

        def first_cuts(cut, first=0, last=2 + G):
            flat = "p c d -> p (c d)"
            for n, (w, raw) in enumerate([(wks, raw_kv[:, 0]), (wvs, raw_kv[:, 1])]
                                         + [(wqs[r], raw_q[:, r]) for r in range(G)]):
                if first <= n < last:
                    cut(w[0][:].rearrange(flat), w[1][:].rearrange(flat), raw.rearrange(flat), n + 1)

        def cuts(g, k, cut):
            flat = "p c d -> p (c d)"
            base = 6 + 10 * g
            if k == 4:
                for r in range(G):
                    n = base + 3 + r if exists(8 * g + k, 0, UNITS - 9) else base + 1 + r
                    cut(wds[r][0][:], wds[r][1][:], raw_d[:, r], n)
            if exists(8 * g + k, 0, UNITS - 9):
                if k == 3:
                    cut(wks[0][:].rearrange(flat), wks[1][:].rearrange(flat), raw_kv[:, 0].rearrange(flat), base + 1)
                    cut(wvs[0][:].rearrange(flat), wvs[1][:].rearrange(flat), raw_kv[:, 1].rearrange(flat), base + 2)
                if 4 <= k <= 7:
                    r = k - 4
                    cut(wqs[r][0][:].rearrange(flat), wqs[r][1][:].rearrange(flat), raw_q[:, r].rearrange(flat),
                        base + 7 + r)

        @block.sync
        def _(sp):
            xv = x_in.rearrange("(t p) h -> p t h", p=P)
            for pair_at, s in enumerate((loaded.x0, loaded.x1, loaded.x2, loaded.x3)):
                part = slice(2 * pair_at, 2 * pair_at + 2)
                sp.dma_start(x[:, part, :], xv[:, part, :]).then_inc(s, 16)
            sp.dma_start(gw_raw[:], gate_w).then_inc(loaded.gate, 16)

            def load_shared(n, e):
                f = ffn[n]
                if e >= 2:
                    sp.wait_ge(f.dn_hi, e - 1)
                    sp.wait_ge(f.dn_lo, e - 1)
                sp.dma_start(raw_w[e % 2][:], ffn_w[NEXP + e]).then_inc(raw_loaded[e % 2], 16)

            def load_tile(n, it, k):
                j = 4 * it + k
                wait(sp, moe[n].x_mm, j - RING + 1)
                sp.dma_start(xn[:, k, :], x_rows[bass.ds(j * P, P), :]).then_inc(tile_in[k], 16)

            def store_tile(n, it, k):
                j = 4 * it + k
                sp.wait_ge(moe[n].y_out, j + 1)
                sp.dma_start(y_rows[bass.ds(j * P, P), :], xn[:, RING + k, :]).then_inc(tile_out[k], 16)

            def feed_forward(n):
                if n == 1:
                    sp.wait_ge(att.pv_mm, UNITS)
                for e in range(2):
                    load_shared(n, e)
                if n == 1:
                    sp.wait_ge(att.o_mm, UNITS)
                if n == 0:
                    sp.wait_ge(consts.zero, 1)
                    sp.dma_start(x_rows.rearrange("(j p) h -> p j h", p=P),
                                 experts[:, (NEXP - 1) * FW:(NEXP - 1) * FW + HID].unsqueeze(1).to_broadcast([P, TILES, HID])
                                 ).then_inc(route[n].cleared, 16)

                def load_expert(e):
                    sp.dma_start(experts[:, e * FW:(e + 1) * FW], ffn_w[e]).then_inc(moe[n].weights, 16)

                for e in range(NEXP // 2):
                    if n == 0 and e == 4:
                        load_shared(n, 2)
                    load_expert(e)
                if n == 1:
                    load_shared(n, 2)
                sp.wait_ge(moe[n].weights, LOADED_HALF)
                if n == 0:
                    sp.wait_ge(route[n].cleared, 16)
                for e in range(NEXP // 2, NEXP // 2 + EARLY[n]):
                    load_expert(e)
                load_shared(n, 3)
                sp.wait_ge(route[n].scattered, 2 * TT * 16)
                for k in range(4):
                    load_tile(n, 0, k)
                left = range(NEXP // 2 + EARLY[n], NEXP)
                for e in left[:1]:
                    load_expert(e)
                load_tile(n, 1, 0)
                for e in left[1:3]:
                    load_expert(e)
                load_tile(n, 1, 1)
                for e in left[3:]:
                    load_expert(e)
                for k in range(4):
                    store_tile(n, 0, k)
                    if k < 2:
                        load_tile(n, 1, k + 2)
                with sp.Fori(2, TILES // 4) as it:
                    for k in range(4):
                        load_tile(n, it, k)
                        store_tile(n, it - 1, k)
                last = TILES // 4
                for k in range(4):
                    if k < TILES % 4:
                        load_tile(n, last, k)
                    store_tile(n, last - 1, k)
                for k in range(TILES % 4):
                    store_tile(n, last, k)

            feed_forward(0)
            sp.wait_ge(moe[0].y_mm, TILES)
            sp.dma_start(raw_kv[:], wkv[0]).then_inc(loaded.kv, 16)
            sp.wait_ge(gathered[HALF - 1], 2 * 16)
            sp.dma_start(raw_q[:], wq[0]).then_inc(loaded.q, 16)
            sp.dma_start(raw_d[:], wd[0]).then_inc(loaded.d, 16)
            with sp.Fori(1, KV) as g:
                wait(sp, att.w_hi, 6 + 10 * (g - 1))
                wait(sp, att.w_lo, 6 + 10 * (g - 1))
                sp.dma_start(raw_kv[:], wkv[bass.ds(g, 1)].rearrange("a p k c d -> (a p) k c d")).then_inc(loaded.kv, 16)
                sp.dma_start(raw_q[:], wq[bass.ds(g, 1)].rearrange("a p r c d -> (a p) r c d")).then_inc(loaded.q, 16)
                wait(sp, att.w_hi, 6 + 10 * (g - 1) + 6)
                wait(sp, att.w_lo, 6 + 10 * (g - 1) + 6)
                sp.dma_start(raw_d[:], wd[bass.ds(g, 1)].rearrange("a p r h -> (a p) r h")).then_inc(loaded.d, 16)
            feed_forward(1)
            for t in range(TT):
                sp.wait_ge(moe[1].added, 4 * (t // 2) + 3 + t % 2)
                sp.wait_ge(ffn[1].added, HALF * (SLOTS - 2) + t + 1)
                sp.dma_start(out[t * P:(t + 1) * P, :], x[:, t, :]).then_inc(stored, 16)
            sp.wait_ge(stored, TT * 16)

        @block.gpsimd
        def _(pool):
            nc.gpsimd.memset(experts[:, (NEXP - 1) * FW:(NEXP - 1) * FW + HID], 0.0).then_inc(consts.zero, 1)
            nc.gpsimd.memset(ident[:], 0.0).then_inc(consts.mem, 1)
            nc.gpsimd.memset(ones[:], 1.0).then_inc(consts.mem, 1)
            nc.gpsimd.memset(below[:], 1.0).then_inc(consts.mem, 1)
            nc.gpsimd.memset(earlier[:], 1.0).then_inc(consts.mem, 1)
            nc.gpsimd.iota(counts_i[:], pattern=[[1, TILES + 3]], base=0, channel_multiplier=0).then_inc(consts.mem, 1)
            pool.wait_ge(consts.mem, 5)
            nc.gpsimd.affine_select(out=ident[:], in_=ident[:], compare_op=ALU.not_equal, fill=1.0, base=0,
                                    pattern=[[-1, P]], channel_multiplier=1).then_inc(consts.ident, 1)
            nc.gpsimd.affine_select(out=below[:], in_=below[:], compare_op=ALU.is_gt, fill=0.0, base=0,
                                    pattern=[[1, P]], channel_multiplier=-1).then_inc(consts.below, 1)
            nc.gpsimd.affine_select(out=earlier[:], in_=earlier[:], compare_op=ALU.is_gt, fill=0.0, base=0,
                                    pattern=[[1, NEXP], [-1, NEXP]], channel_multiplier=0).then_inc(consts.earlier, 1)
            nc.gpsimd.tensor_copy(counts[:], counts_i[:]).then_inc(consts.counts, 1)

            def low_gu(n, e):
                pool.wait_ge(ffn[n].gu_hi, e + 1)
                nc.gpsimd.tensor_tensor(wgu[1][:].rearrange("p c k i -> p (c k i)"), raw_w[e % 2][:, 0:GU],
                                        wgu[0][:].bitcast(F32).rearrange("p c k i -> p (c k i)"),
                                        ALU.subtract).then_inc(ffn[n].gu_lo, 1)

            def low_dn(n, e):
                pool.wait_ge(ffn[n].dn_hi, e + 1)
                nc.gpsimd.tensor_tensor(wdn[1][:], raw_w[e % 2][:, GU:FW], wdn[0][:].bitcast(F32),
                                        ALU.subtract).then_inc(ffn[n].dn_lo, 1)

            def routed(n):
                base = n * TILES

                def back(par, at, count):
                    pool.wait_ge(tile_part.back_hi, base + count)
                    nc.gpsimd.tensor_tensor(tback[par][1][:, FRONT:], experts[:, bass.ds(at + 2 * FRONT, GU - 2 * FRONT)],
                                            tback[par][0][:, FRONT:].bitcast(F32),
                                            ALU.subtract).then_inc(tile_part.back_lo, 1)

                def step(it, k, at, there):
                    j, par = 4 * it + k, k % 2
                    if exists(j, 0, TILES - 2):
                        back(1 - par, at[k + 1], j + 2)
                    if exists(j, 0, TILES - 1):
                        pool.wait_ge(tile_part.dn_hi, base + j + 1)
                        nc.gpsimd.tensor_tensor(tdn[par][1][:], experts[:, bass.ds(at[k] + GU, HID)],
                                                tdn[par][0][:].bitcast(F32),
                                                ALU.subtract).then_inc(tile_part.dn_lo, 1)

                low_gu(n, NSH - 1)
                back(0, places(pool, 0)[0][0], 1)
                low_dn(n, NSH - 1)
                tile_steps(pool, step)

            def feed_forward(n):
                low_gu(n, 0)
                pool.wait_ge(route[n].rows, 1)
                if n == 0:
                    pool.wait_ge(route[n].cleared, 16)
                for t in range(TT):
                    for m in range(2):
                        nc.gpsimd.indirect_dma_start(
                            out=x_rows, out_offset=bass.IndirectOffsetOnAxis(ap=rows[:, t, m:m + 1], axis=0),
                            in_=xn[:, t, :], in_offset=None).then_inc(route[n].scattered, 16)
                routed(n)
                for k in range(RING):
                    pool.wait_ge(tile_out[k], copies(n + 1, k, 0))
                pool.wait_ge(moe[n].y_mm, TILES)
                for t in range(TT):
                    for m in range(2):
                        nc.gpsimd.indirect_dma_start(
                            out=yg[:, t, m, :], out_offset=None, in_=y_rows,
                            in_offset=bass.IndirectOffsetOnAxis(ap=rows[:, t, m:m + 1], axis=0)
                        ).then_inc(gathered[t], 16)

            def slot(g, k):
                u = 8 * g + k
                r = k % 4
                if exists(u, 0, UNITS - 1):
                    for i in (3, 2, 0, 1):
                        if i == 3:
                            wait(pool, att.inv, u + 1)
                        s = sp_[k % 2][:, TRI[i]:TRI[i + 1]]
                        nc.gpsimd.tensor_tensor(s, s, pinv[k % 2][:, i:i + 1].to_broadcast([P, P * (i + 1)]),
                                                ALU.mult).then_inc(att.normed, 1)
                cuts(g, k, low_part)

            def low_part(hi, lo, raw, count):
                wait(pool, att.w_hi, count)
                nc.gpsimd.tensor_tensor(lo, raw, hi.bitcast(F32), ALU.subtract).then_inc(att.w_lo, 1)

            feed_forward(0)
            pool.wait_ge(moe[0].y_mm, TILES)
            first_cuts(low_part)
            nc.gpsimd.memset(causal[:], 0.0).then_inc(consts.causal0, 1)
            pool.wait_ge(consts.causal0, 1)
            nc.gpsimd.affine_select(out=causal[:, 384:512], in_=causal[:, 384:512], compare_op=ALU.is_ge, fill=MASKED,
                                    base=0, pattern=[[-1, P]], channel_multiplier=1).then_inc(consts.causal, 1)
            att_slots(pool, slot)
            feed_forward(1)

        @block.scalar
        def _(act):
            def roots(n, h):
                act.wait_ge(norm[n].var, h + 1)
                part = slice(HALF * h, HALF * h + HALF)
                nc.scalar.activation(root[:, part], rvar[:, part], ACT.Sqrt).then_inc(norm[n].root, 1)

            def turned_norm(n, h):
                for t in range(HALF * h, HALF * h + HALF):
                    act.wait_ge(norm[n].transposed, t + 1)
                    nc.scalar.activation(xnT[0][:, :, t * P:(t + 1) * P],
                                         bank[norm_bank(n, t)][:].rearrange("p (c t) -> p c t", c=HC),
                                         ACT.Copy).then_inc(norm[n].hi, 1)

            def router(n):
                for b in range(BATCH):
                    act.wait_ge(route[n].logits, b + 1)
                    nc.scalar.activation(logT[b], bank[1 + 2 * b][0:NEXP, :],
                                         ACT.Copy).then_inc(route[n].out, 1)
                act.wait_ge(route[n].sub, 1)
                nc.scalar.activation(lexp[:], lsub[:], ACT.Exp).then_inc(route[n].exp, 1)

            def cut_gu(n, e):
                f = ffn[n]
                act.wait_ge(raw_loaded[e % 2], 16 * (n * NSH // 2 + e // 2 + 1))
                wait(act, f.u_mm, 2 * e)
                nc.scalar.activation(wgu[0][:].rearrange("p c k i -> p (c k i)"), raw_w[e % 2][:, 0:GU],
                                     ACT.Copy).then_inc(f.gu_hi, 1)

            def cut_dn(n, e):
                f = ffn[n]
                wait(act, f.d_mm, 4 * 2 * e)
                nc.scalar.activation(wdn[0][:], raw_w[e % 2][:, GU:FW], ACT.Copy).then_inc(f.dn_hi, 1)

            def shared(n, first, last):
                f = ffn[n]
                for s in range(first, last):
                    par = s % 2
                    act.wait_ge(f.g_mm, s + 1)
                    wait(act, f.act_lo, s - 1)
                    if s == 1:
                        act.wait_ge(route[n].turned, 1)
                    nc.scalar.activation(sg[par][:], bank[par][:], ACT.Silu).then_inc(f.silu, 1)
                    if s % 2 and s // 2 + 1 < NSH:
                        cut_gu(n, s // 2 + 1)
                    act.wait_ge(f.mul, s + 1)
                    wait(act, f.d_mm, 4 * (s - 1))
                    nc.scalar.activation(ab[par][0][:], sg[par][:], ACT.Copy).then_inc(f.act_hi, 1)
                    if s % 2 == 0 and s and s != BEFORE:
                        cut_dn(n, s // 2)

            def routed(n):
                m = moe[n]

                base = n * TILES

                def turned(par, count):
                    act.wait_ge(m.x_mm, count)
                    nc.scalar.activation(xT[par][0][:].rearrange("p c t -> p (c t)"), bank[2 + par][:],
                                         ACT.Copy).then_inc(m.x_out, 1)

                def front(at):
                    nc.scalar.activation(tfront[0][:], experts[:, bass.ds(at, FRONT)],
                                         ACT.Copy).then_inc(tile_part.front_hi, 1)

                def back(par, at, there):
                    act.wait_ge(m.weights, there)
                    nc.scalar.activation(tback[par][0][:], experts[:, bass.ds(at + FRONT, GU - FRONT)],
                                         ACT.Copy).then_inc(tile_part.back_hi, 1)

                def step(it, k, at, there):
                    j, par = 4 * it + k, k % 2
                    if exists(j, 0, TILES - 2):
                        wait(act, m.gu_mm, j)
                        back(1 - par, at[k + 1], there[k + 1])
                    if exists(j, 1, TILES):
                        act.wait_ge(m.h_mm, j)
                        nc.scalar.activation(hT[0][:], bank[4 + 1 - par][:, 0:P],
                                             ACT.Copy).then_inc(m.h_out, 1)
                    if exists(j, 0, TILES - 2):
                        turned(1 - par, j + 2)
                        act.wait_ge(tile_part.front_mm, base + j + 1)
                        front(at[k + 1])
                    if exists(j, 0, TILES - 1):
                        act.wait_ge(m.gu_mm, j + 1)
                        nc.scalar.activation(ht[:], bank[par][:, 0:INTER], ACT.Silu).then_inc(m.silu, 1)
                        if isinstance(j, int) and j == 0:
                            act.wait_ge(ffn[n].dn_lo, NSH)
                        wait(act, m.y_mm, j - 1)
                        nc.scalar.activation(tdn[par][0][:], experts[:, bass.ds(at[k] + GU, HID)],
                                             ACT.Copy).then_inc(tile_part.dn_hi, 1)

                act.wait_ge(route[n].rows, 1)
                at, there = places(act, 0, loads=True)
                back(0, at[0], there[0])
                act.wait_ge(ffn[n].dn_lo, NSH - 1)
                front(at[0])
                turned(0, 1)
                cut_dn(n, BEFORE // 2)
                tile_steps(act, step, loads=True)

            def attention():
                def high_part(hi, lo, raw, count):
                    nc.scalar.activation(hi, raw, ACT.Copy).then_inc(att.w_hi, 1)

                def high_parts(g, k):
                    u = 8 * g + k
                    if k == 3 and exists(u, 0, UNITS - 9):
                        act.wait_ge(loaded.kv, 16 * (g + 2))
                        act.wait_ge(att.proj_mm, PROJ_AHEAD + 7 * (2 * g) + XPOS[2] + 1)
                    if 4 <= k <= 7 and exists(u, 0, UNITS - 9):
                        act.wait_ge(loaded.q, 16 * (g + 2))
                        act.wait_ge(att.proj_mm, PROJ_AHEAD + 7 * (2 * g + (k - 1) // 4) + QPOS[(k - 1) % 4] + 1)
                    if k == 4:
                        act.wait_ge(loaded.d, 16 * (g + 1))
                        wait(act, att.o_mm, u - 4)
                    cuts(g, k, high_part)

                def turned_hi(u, n, lo_col, hi_col, b):
                    act.wait_ge(att.t_mm, 3 * u + n + 1)
                    if n == 0:
                        wait(act, att.pv_mm, u)
                    nc.scalar.activation(pT[0][:, lo_col:hi_col], bank[b][:, 0:hi_col - lo_col],
                                         ACT.Copy).then_inc(att.t_hi, 1)

                def slot(g, k):
                    u, par, r, b = 8 * g + k, k % 2, k % 4, (k // 4) % 2
                    quad = 2 * g + k // 4
                    if exists(u, 1, UNITS):
                        turned_hi(u - 1, 0, COL[0], COL[1], 6)
                        turned_hi(u - 1, 1, COL[1], COL[2], 7)
                    if exists(u, 0, UNITS - 1):
                        for n, i in enumerate((3, 2, 0, 1)):
                            act.wait_ge(att.masked, 4 * u + n + 1)
                            s = sp_[par][:, TRI[i]:TRI[i + 1]]
                            nc.scalar.activation(s, s, ACT.Exp, bias=nmax[par][:, i:i + 1], scale=-1.0,
                                                 accum_out=psumr[par][:, i:i + 1]).then_inc(att.exp, 1)
                    if exists(u, 1, UNITS):
                        turned_hi(u - 1, 2, COL[2], TRI[ST], 6)
                    if exists(u, 0, UNITS - 2):
                        act.wait_ge(att.proj_mm, PROJ_AHEAD + 7 * quad + qpos(u, r) + 1)
                        nc.scalar.activation(qT[0][:], bank[0][:], ACT.Copy).then_inc(att.proj_hi, 1)
                    if exists(u, 1, UNITS):
                        ru, bu = (k - 1) % 4, ((k - 1) // 4) % 2
                        act.wait_ge(att.pv_mm, u)
                        wait(act, att.o_mm, u - 1 - ru - 4)
                        nc.scalar.activation(oT[bu][ru][0][:], bank[1][:], ACT.Copy).then_inc(att.pv_hi, 1)
                    if isinstance(u, int) and u == 0:
                        roots(1, 1)
                    if isinstance(u, int) and u == 1:
                        turned_norm(1, 1)
                    if r in (1, 3) and exists(u, 0, UNITS - 5):
                        act.wait_ge(att.proj_mm, PROJ_AHEAD + 7 * quad + XPOS[r] + 1)
                        if r == 1:
                            nc.scalar.activation(kT[1 - b][0][:], bank[0][:], ACT.Copy).then_inc(att.proj_hi, 1)
                        else:
                            nc.scalar.activation(vv[1 - b][0][:].rearrange("p c d -> p (c d)"), bank[0][:],
                                                 ACT.Copy).then_inc(att.proj_hi, 1)
                    if k < 8:
                        high_parts(g, k)

                act.wait_ge(loaded.kv, 16)
                first_cuts(high_part, 0, 2)
                act.wait_ge(loaded.q, 16)
                first_cuts(high_part, 2, 3)
                roots(1, 0)
                first_cuts(high_part, 3)
                turned_norm(1, 0)
                for n, dst, b in ((1, kT[0][0][:], 0), (3, qT[0][:], 4),
                                  (4, vv[0][0][:].rearrange("p c d -> p (c d)"), 0)):
                    act.wait_ge(att.proj_mm, n)
                    nc.scalar.activation(dst, bank[b][:], ACT.Copy).then_inc(att.proj_hi, 1)
                att_slots(act, slot)

            def feed_forward(n):
                roots(2 * n, 0)
                if n == 1:
                    act.wait_ge(att.o_mm, UNITS)
                if n == 0:
                    act.wait_ge(loaded.gate, 16)
                    nc.scalar.activation(gw[0][:], gw_raw[:], ACT.Copy).then_inc(route[n].gate_hi, 1)
                cut_gu(n, 0)
                turned_norm(2 * n, 0)
                roots(2 * n, 1)
                cut_dn(n, 0)
                turned_norm(2 * n, 1)
                shared(n, 0, 1)
                router(n)
                shared(n, 1, BEFORE)
                routed(n)
                shared(n, BEFORE, SLOTS)

            feed_forward(0)
            attention()
            feed_forward(1)

        @block.vector
        def _(dve):
            def statistics(n, h):
                s = norm[n]
                part = slice(HALF * h, HALF * h + HALF)
                count = [(2 * HALF + 5) * (n * BATCH + h)]

                def then(ins):
                    count[0] += 1
                    ins.then_inc(norm_chain, 1)
                    dve.wait_ge(norm_chain, count[0])

                if n == 1:
                    dve.wait_ge(moe[0].added, 2 * HALF * (h + 1))
                if n == 2:
                    dve.wait_ge(att.added, UNITS - HALF * (1 - h))
                for t in range(HALF * h, HALF * h + HALF):
                    if n == 0 and t % 2 == 0:
                        dve.wait_ge((loaded.x0, loaded.x1, loaded.x2, loaded.x3)[t // 2], 16)
                    nc.vector.bn_stats(stats[:, t, :], x[:, t, :]).then_inc(norm_chain, 1)
                    count[0] += 1
                for t in range(HALF * h, HALF * h + HALF):
                    dve.wait_ge(norm_chain, count[0] - HALF + 1 + t % HALF)
                    nc.vector.bn_aggr(mv[:, t, :], stats[:, t, :]).then_inc(norm_chain, 1)
                count[0] += HALF
                dve.wait_ge(norm_chain, count[0])
                then(nc.vector.tensor_scalar(veps[:, part], mv[:, part, 1], EPS, None, ALU.add))
                nc.vector.reciprocal(rvar[:, part], veps[:, part]).then_inc(s.var, 1)
                return then

            def scaled(n, h, then):
                s = norm[n]
                part = slice(HALF * h, HALF * h + HALF)
                dve.wait_ge(s.root, h + 1)
                then(nc.vector.tensor_tensor(newt[:, part], root[:, part], root[:, part], ALU.mult))
                then(nc.vector.tensor_tensor(newt[:, part], newt[:, part], veps[:, part], ALU.mult))
                then(nc.vector.tensor_scalar(newt[:, part], newt[:, part], -0.5, 1.5, ALU.mult, ALU.add))
                then(nc.vector.tensor_tensor(rstd[:, part], newt[:, part], root[:, part], ALU.mult))
                for t in range(HALF * h, HALF * h + HALF):
                    nc.vector.tensor_scalar(xn[:, t, :], x[:, t, :], mv[:, t, 0:1], rstd[:, t:t + 1], ALU.subtract,
                                            ALU.mult).then_inc(s.mul, 1)

            def normalise(n, h):
                scaled(n, h, statistics(n, h))

            def turned_norm(n, h):
                s = norm[n]
                for t in range(HALF * h, HALF * h + HALF):
                    dve.wait_ge(s.hi, t + 1)
                    nc.vector.tensor_tensor(xnT[1][:, :, t * P:(t + 1) * P],
                                            bank[norm_bank(n, t)][:].rearrange("p (c t) -> p c t", c=HC),
                                            xnT[0][:, :, t * P:(t + 1) * P].bitcast(F32),
                                            ALU.subtract).then_inc(s.lo, 1)

            def router(n):
                s = route[n]
                count = [0]

                def then(ins):
                    count[0] += 1
                    ins.then_inc(s.chain, 1)
                    dve.wait_ge(s.chain, count[0])

                logits = bank[7][:, 0:TT * NEXP].rearrange("p (t e) -> p t e", e=NEXP)
                dve.wait_ge(s.turned, 1)
                then(nc.vector.tensor_reduce(lmax[:], logits, AX_X, ALU.max))
                nc.vector.tensor_tensor(lsub[:], logits, lmax[:].unsqueeze(2).to_broadcast([P, TT, NEXP]),
                                        ALU.subtract).then_inc(s.sub, 1)
                dve.wait_ge(s.exp, 1)
                then(nc.vector.tensor_reduce(lsum[:], lexp[:], AX_X, ALU.add))
                then(nc.vector.reciprocal(lrec[:], lsum[:]))
                then(nc.vector.tensor_tensor(prob[:], lexp[:], lrec[:].unsqueeze(2).to_broadcast([P, TT, NEXP]),
                                             ALU.mult))
                for t in range(TT):
                    last = nc.vector.max(top8[:, t, :], prob[:, t, :])
                then(last)
                for t in range(TT):
                    last = nc.vector.max_index(idx8[:, t, :], top8[:, t, :], prob[:, t, :])
                then(last)
                then(nc.vector.tensor_copy(idxf[:], idx8[:]))
                then(nc.vector.tensor_tensor(tsum[:], top8[:, :, 0], top8[:, :, 1], ALU.add))
                then(nc.vector.reciprocal(trec[:], tsum[:]))
                then(nc.vector.tensor_scalar(trec[:], trec[:], 0.5, None, ALU.mult))
                then(nc.vector.tensor_tensor(wtop[:], top8[:, :, 0:2], trec[:].unsqueeze(2).to_broadcast([P, TT, 2]),
                                             ALU.mult))
                dve.wait_ge(consts.counts, 1)
                for m in range(2):
                    then(nc.vector.tensor_tensor(hot[:, m], counts[:, 0:NEXP].unsqueeze(1).to_broadcast([P, TT, NEXP]),
                                                 idxf[:, :, m:m + 1].to_broadcast([P, TT, NEXP]), ALU.is_equal))
                nc.vector.tensor_tensor(chosen[:], hot[:, 0], hot[:, 1], ALU.add).then_inc(s.chosen, 1)
                return then

            def place(n, then):
                s = route[n]
                rank = bank[3][:, 0:TT * NEXP].rearrange("p (t e) -> p t e", e=NEXP)
                total = bank[3][:, TT * NEXP:(TT + 1) * NEXP]
                dve.wait_ge(s.ranked, 1)
                then(nc.vector.tensor_scalar(tsum[:], counts[:, 0:TT], float(P), None, ALU.mult))
                then(nc.vector.tensor_tensor(wide[:, 0:TT, :], total.unsqueeze(1).to_broadcast([P, TT, NEXP]),
                                             tsum[:].unsqueeze(2).to_broadcast([P, TT, NEXP]), ALU.is_gt))
                then(nc.vector.tensor_reduce(ntile[:], wide[:, 0:TT, :].rearrange("p t e -> p e t"), AX_X, ALU.add))
                then(nc.vector.tensor_tensor(wide[:, 0:NEXP, :], earlier[:],
                                             ntile[:].unsqueeze(1).to_broadcast([P, NEXP, NEXP]), ALU.mult))
                then(nc.vector.tensor_reduce(ahead[:], wide[:, 0:NEXP, :], AX_X, ALU.add))
                then(nc.vector.tensor_tensor(upto[:], ahead[:], ntile[:], ALU.add))
                then(nc.vector.tensor_scalar(ahead[:], ahead[:], float(P), None, ALU.mult))
                then(nc.vector.tensor_tensor(spot[:], rank, ahead[:].unsqueeze(1).to_broadcast([P, TT, NEXP]), ALU.add))
                then(nc.vector.tensor_tensor(hot[:], hot[:], spot[:].unsqueeze(1).to_broadcast([P, 2, TT, NEXP]),
                                             ALU.mult))
                then(nc.vector.tensor_reduce(rowf[:], hot[:], AX_X, ALU.add))
                then(nc.vector.tensor_copy(rows[:].rearrange("p t m -> p m t"), rowf[:]))
                then(nc.vector.tensor_tensor(wide[0:1], counts[0:1].unsqueeze(2).to_broadcast([1, TILES + 3, NEXP]),
                                             upto[0:1].unsqueeze(1).to_broadcast([1, TILES + 3, NEXP]), ALU.is_gt))
                then(nc.vector.tensor_reduce(tilef[:], wide[0:1], AX_X, ALU.add))
                then(nc.vector.tensor_scalar(tilef[:], tilef[:], float(NEXP - 1), None, ALU.min))
                span = RING * (WORDS - 1) + 1
                then(nc.vector.tensor_copy(wordf[:], tilef[:, 1:1 + span:RING]))
                for m in range(1, RING + 1):
                    then(nc.vector.scalar_tensor_tensor(out=wordf[:], in0=tilef[:, 1 + m:1 + m + span:RING],
                                                        scalar=float(NEXP ** m), in1=wordf[:], op0=ALU.mult,
                                                        op1=ALU.add))
                nc.vector.tensor_copy(tile_w[:], wordf[:]).then_inc(s.rows, 1)

            def low_gu(n, e):
                dve.wait_ge(ffn[n].gu_hi, e + 1)
                nc.vector.tensor_tensor(wgu[1][:].rearrange("p c k i -> p (c k i)"), raw_w[e % 2][:, 0:GU],
                                        wgu[0][:].bitcast(F32).rearrange("p c k i -> p (c k i)"),
                                        ALU.subtract).then_inc(ffn[n].gu_lo, 1)

            def low_dn(n, e):
                dve.wait_ge(ffn[n].dn_hi, e + 1)
                nc.vector.tensor_tensor(wdn[1][:], raw_w[e % 2][:, GU:FW], wdn[0][:].bitcast(F32),
                                        ALU.subtract).then_inc(ffn[n].dn_lo, 1)

            def add_down(n, s):
                f = ffn[n]
                for t in range(HALF):
                    tile = HALF * (s % 2) + t
                    dve.wait_ge(f.d_mm, HALF * s + t + 1)
                    wait(dve, f.added, HALF * (s - 2) + t + 1)
                    if s == SLOTS - 2 and t < 2:
                        dve.wait_ge(moe[n].added, 3 + t)
                    nc.vector.scalar_tensor_tensor(out=x[:, tile, :], in0=bank[4 + t][:], scalar=0.5,
                                                   in1=x[:, tile, :], op0=ALU.mult, op1=ALU.add).then_inc(f.added, 1)

            def shared(n, first, last):
                f = ffn[n]
                for s in range(first, last):
                    par = s % 2
                    dve.wait_ge(f.silu, s + 1)
                    dve.wait_ge(f.u_mm, s + 1)
                    nc.vector.tensor_tensor(sg[par][:], sg[par][:], bank[2 + par][:], ALU.mult).then_inc(f.mul, 1)
                    if s % 2 and s // 2 + 1 < NSH and s != BEFORE - 1:
                        low_gu(n, s // 2 + 1)
                    dve.wait_ge(f.act_hi, s + 1)
                    nc.vector.tensor_tensor(ab[par][1][:], sg[par][:], ab[par][0][:].bitcast(F32),
                                            ALU.subtract).then_inc(f.act_lo, 1)
                    if s and s != BEFORE:
                        add_down(n, s - 1)
                    if s % 2 == 0 and s and s != BEFORE:
                        low_dn(n, s // 2)

            def routed(n):
                m = moe[n]

                base = n * TILES

                def turned(par, count):
                    dve.wait_ge(m.x_out, count)
                    nc.vector.tensor_tensor(xT[par][1][:].rearrange("p c t -> p (c t)"), bank[2 + par][:],
                                            xT[par][0][:].bitcast(F32).rearrange("p c t -> p (c t)"),
                                            ALU.subtract).then_inc(tile_part.x_lo, 1)

                def front(at, count):
                    dve.wait_ge(tile_part.front_hi, base + count)
                    nc.vector.tensor_tensor(tfront[1][:], experts[:, bass.ds(at, FRONT)],
                                            tfront[0][:].bitcast(F32), ALU.subtract).then_inc(tile_part.front_lo, 1)

                def middle(par, at, count):
                    dve.wait_ge(tile_part.back_hi, base + count)
                    nc.vector.tensor_tensor(tback[par][1][:, 0:FRONT], experts[:, bass.ds(at + FRONT, FRONT)],
                                            tback[par][0][:, 0:FRONT].bitcast(F32),
                                            ALU.subtract).then_inc(tile_part.middle_lo, 1)

                def step(it, k, at, there):
                    j, par = 4 * it + k, k % 2
                    if exists(j, 1, TILES):
                        dve.wait_ge(m.h_out, j)
                        nc.vector.tensor_tensor(hT[1][:], bank[4 + 1 - par][:, 0:P],
                                                hT[0][:].bitcast(F32),
                                                ALU.subtract).then_inc(tile_part.h_lo, 1)
                    if exists(j, 0, TILES - 2):
                        turned(1 - par, j + 2)
                        front(at[k + 1], j + 2)
                    if exists(j, 0, TILES - 1):
                        dve.wait_ge(m.silu, j + 1)
                        nc.vector.tensor_tensor(ht[:], ht[:], bank[par][:, INTER:2 * INTER],
                                                ALU.mult).then_inc(m.mul, 1)
                    if exists(j, 0, TILES - 2):
                        middle(1 - par, at[k + 1], j + 2)
                    if exists(j, 1, TILES):
                        dve.wait_ge(m.y_mm, j)
                        if exists(j, RING + 1, TILES):
                            dve.wait_ge(tile_out[(k - 1) % 4], copies(n, (k - 1) % 4, it + (k - 1) // 4))
                        nc.vector.tensor_copy(xn[:, RING + (k - 1) % 4, :], bank[6 + 1 - par][:]).then_inc(m.y_out, 1)

                at = places(dve, 0)[0]
                middle(0, at[0], 1)
                front(at[0], 1)
                turned(0, 1)
                add_down(n, BEFORE - 1)
                dve.wait_ge(route[n].scattered, 2 * TT * 16)
                tile_steps(dve, step)

            def combine(n, t):
                for m in range(2):
                    for tile in (t, t + 1):
                        if m == 0:
                            dve.wait_ge(gathered[tile], 2 * 16 * (n + 1))
                            dve.wait_ge(ffn[n].added, HALF * (SLOTS - 4) + tile + 1 if t == 0 else
                                        HALF * (SLOTS - 2) + tile + 1)
                        wait(dve, moe[n].added, 2 * t + 2 * m - 1 + tile - t)
                        nc.vector.scalar_tensor_tensor(out=x[:, tile, :], in0=yg[:, tile, m, :],
                                                       scalar=wtop[:, tile, m:m + 1], in1=x[:, tile, :],
                                                       op0=ALU.mult, op1=ALU.add).then_inc(moe[n].added, 1)

            def attention():
                def turned_lo(u, n, lo_col, hi_col, b):
                    dve.wait_ge(att.t_hi, 3 * u + n + 1)
                    nc.vector.tensor_tensor(pT[1][:, lo_col:hi_col], bank[b][:, 0:hi_col - lo_col],
                                            pT[0][:, lo_col:hi_col].bitcast(F32), ALU.subtract).then_inc(att.t_lo, 1)

                def low(dst, src, hi, s):
                    nc.vector.tensor_tensor(dst, src, hi.bitcast(F32), ALU.subtract).then_inc(s, 1)

                after_statistics = []

                def slot(g, k):
                    u, par, r, b = 8 * g + k, k % 2, k % 4, (k // 4) % 2
                    quad = 2 * g + k // 4
                    if exists(u, 0, UNITS - 1):
                        for n, (i, bk, c) in enumerate(((3, 3, 0), (2, 4, 0), (0, 4, 384), (1, 5, 0))):
                            if n != 2:
                                dve.wait_ge(att.s_mm, 3 * u + (0, 1, 1, 2)[n] + 1)
                                nc.vector.memset(idle[:, n:n + 1], 0.0)
                            w = P * (i + 1)
                            nc.vector.tensor_tensor_reduce(sp_[par][:, TRI[i]:TRI[i + 1]], bank[bk][:, c:c + w],
                                                           causal[:, 512 - w:512], -SCORE_SCALE, 3.0e38, ALU.add,
                                                           ALU.min, nmax[par][:, i:i + 1]).then_inc(att.masked, 1)
                    if exists(u, 1, UNITS):
                        turned_lo(u - 1, 0, COL[0], COL[1], 6)
                        turned_lo(u - 1, 1, COL[1], COL[2], 7)
                    if isinstance(u, int) and u == 1:
                        scaled(1, 1, after_statistics[0])
                    if exists(u, 0, UNITS - 1):
                        dve.wait_ge(att.exp, 4 * u + 4)
                        nc.vector.reciprocal(pinv[par][:], psumr[par][:]).then_inc(att.inv, 1)
                    if exists(u, 1, UNITS):
                        turned_lo(u - 1, 2, COL[2], TRI[ST], 6)
                    if exists(u, 0, UNITS - 2):
                        dve.wait_ge(att.proj_hi, 3 + 6 * quad + qpos(u, r, (0, 1, 3, 4)) + 1)
                        low(qT[1][:], bank[0][:], qT[0][:], att.proj_out)
                    if exists(u, 5, UNITS + 4):
                        tile = (3, 4, 5, 6, 7, 0, 1, 2)[k % 8]
                        dve.wait_ge(att.o_mm, u - 4)
                        nc.vector.tensor_tensor(x[:, tile, :], o_bank(u)[:], x[:, tile, :], ALU.add).then_inc(att.added, 1)
                    if exists(u, 1, UNITS):
                        ru, bu = (k - 1) % 4, ((k - 1) // 4) % 2
                        dve.wait_ge(att.pv_hi, u)
                        low(oT[bu][ru][1][:], bank[1][:], oT[bu][ru][0][:], att.pv_lo)
                    if isinstance(u, int) and u == 0:
                        after_statistics.append(statistics(1, 1))
                    if isinstance(u, int) and u == 1:
                        turned_norm(1, 1)
                    if exists(u, 0, UNITS - 5):
                        if r == 1:
                            dve.wait_ge(att.proj_hi, 3 + 6 * quad + 2 + 1)
                            low(kT[1 - b][1][:], bank[0][:], kT[1 - b][0][:], att.proj_out)
                        if r == 2:
                            dve.wait_ge(att.proj_mm, PROJ_AHEAD + 7 * quad + XPOS[2] + 1)
                            nc.vector.tensor_copy(vT[:], bank[0][:]).then_inc(att.proj_out, 1)
                        if r == 3:
                            dve.wait_ge(att.proj_hi, 3 + 6 * quad + 5 + 1)
                            low(vv[1 - b][1][:].rearrange("p c d -> p (c d)"), bank[0][:],
                                vv[1 - b][0][:].rearrange("p c d -> p (c d)"), att.proj_out)

                dve.wait_ge(consts.causal, 1)
                dve.wait_ge(att.proj_hi, 1)
                low(kT[0][1][:], bank[0][:], kT[0][0][:], att.proj_out)
                dve.wait_ge(att.proj_mm, 2)
                nc.vector.tensor_copy(vT[:], bank[3][:]).then_inc(att.proj_out, 1)
                dve.wait_ge(att.proj_hi, 2)
                low(qT[1][:], bank[4][:], qT[0][:], att.proj_out)
                dve.wait_ge(att.proj_hi, 3)
                low(vv[0][1][:].rearrange("p c d -> p (c d)"), bank[0][:],
                    vv[0][0][:].rearrange("p c d -> p (c d)"), att.proj_out)
                att_slots(dve, slot)
                normalise(2, 0)
                att_tail(slot)

            def feed_forward(n):
                if n == 0:
                    normalise(2 * n, 0)
                turned_norm(2 * n, 0)
                if n == 0:
                    dve.wait_ge(route[n].gate_hi, 1)
                    nc.vector.tensor_tensor(gw[1][:], gw_raw[:], gw[0][:].bitcast(F32),
                                            ALU.subtract).then_inc(route[n].gate_lo, 1)
                normalise(2 * n, 1)
                turned_norm(2 * n, 1)
                low_dn(n, 0)
                shared(n, 0, 1)
                then = router(n)
                shared(n, 1, 2)
                place(n, then)
                shared(n, 2, BEFORE)
                routed(n)
                shared(n, BEFORE, SLOTS - 1)
                combine(n, 0)
                shared(n, SLOTS - 1, SLOTS)
                combine(n, 2)

            feed_forward(0)
            normalise(1, 0)
            turned_norm(1, 0)
            add_down(0, SLOTS - 1)
            combine(0, 4)
            combine(0, 6)
            attention()
            feed_forward(1)
            add_down(1, SLOTS - 1)
            combine(1, 4)
            combine(1, 6)

        @block.tensor
        def _(pe):
            def turn_norm(n, h):
                if n == 0:
                    pe.wait_ge(consts.ident, 1)
                for t in range(HALF * h, HALF * h + HALF):
                    pe.wait_ge(norm[n].mul, t + 1)
                    wait(pe, norm[n].lo, t - 1 if n == 1 and h == 1 else t - 3)
                    for c in range(HC):
                        last = nc.tensor.transpose(bank[norm_bank(n, t)][:, c * P:(c + 1) * P], xn[:, t, c * P:(c + 1) * P],
                                                   ident[:])
                    last.then_inc(norm[n].transposed, 1)

            def router(n):
                if n == 0:
                    pe.wait_ge(route[n].gate_lo, 1)
                for b in range(BATCH):
                    pe.wait_ge(norm[2 * n].lo, HALF * (b + 1))
                    m = 0
                    for c in range(HC):
                        for a, z in PARTS:
                            last = nc.tensor.matmul(bank[1 + 2 * b][0:NEXP, :], gw[a][:, c, :],
                                                    xnT[z][:, c, b * SEQ:(b + 1) * SEQ],
                                                    start=(m == 0), stop=(m == 3 * HC - 1))
                            m += 1
                    last.then_inc(route[n].logits, 1)
                for t in range(TT):
                    if t % HALF == 0:
                        pe.wait_ge(route[n].out, t // HALF + 1)
                    last = nc.tensor.transpose(bank[7][:, t * NEXP:(t + 1) * NEXP], logT[t // HALF][:, t % HALF * P:(t % HALF + 1) * P],
                                               ident[0:NEXP, 0:NEXP])
                last.then_inc(route[n].turned, 1)

            def gate_up(n, s):
                f, tb, par = ffn[n], s % 2, s % 2
                pe.wait_ge(f.gu_lo, s // 2 + 1)
                pe.wait_ge(norm[2 * n].lo, HALF * (tb + 1))
                wait(pe, f.mul, s - 1)
                for half, done in ((0, f.g_mm), (1, f.u_mm)):
                    if half == 1 and s == 3:
                        pe.wait_ge(route[n].rows, 1)
                    m = 0
                    for c in range(HC):
                        for a, b in PARTS:
                            last = nc.tensor.matmul(bank[2 * half + par][:], wgu[a][:, c, half, :],
                                                    xnT[b][:, c, tb * SEQ:(tb + 1) * SEQ],
                                                    start=(m == 0), stop=(m == 3 * HC - 1))
                            m += 1
                    last.then_inc(done, 1)

            def down(n, s):
                f = ffn[n]
                pe.wait_ge(f.dn_lo, s // 2 + 1)
                pe.wait_ge(f.act_lo, s + 1)
                for t in range(HALF):
                    wait(pe, f.added, HALF * (s - 1) + t + 1)
                    if s == 0 and t == 3:
                        pe.wait_ge(route[n].sub, 1)
                    for m, (a, b) in enumerate(PARTS):
                        last = nc.tensor.matmul(bank[4 + t][:], ab[s % 2][a][:, t * P:(t + 1) * P],
                                                wdn[b][:], start=(m == 0), stop=(m == 2))
                    last.then_inc(f.d_mm, 1)

            def rank(n):
                pe.wait_ge(route[n].chosen, 1)
                pe.wait_ge(consts.earlier, 1)
                pe.wait_ge(ffn[n].mul, 2)
                flat = chosen[:].rearrange("p t e -> p (t e)")
                nc.tensor.matmul(bank[3][:, 0:TT * NEXP], below[:], flat, start=True, stop=False,
                                 skip_group_check=True)
                for t in range(TT):
                    last = nc.tensor.matmul(bank[3][:, (t + 1) * NEXP:(TT + 1) * NEXP], ones[:],
                                            chosen[:, t, :].unsqueeze(1).to_broadcast([P, TT - t, NEXP]),
                                            start=False, stop=(t == TT - 1), skip_group_check=True)
                last.then_inc(route[n].ranked, 1)

            def turn(n, k, it, par, count):
                pe.wait_ge(tile_in[k], copies(n, k, it + 1))
                wait(pe, tile_part.x_lo, n * TILES + count - 2)
                for c in range(HC):
                    last = nc.tensor.transpose(bank[2 + par][:, c * P:(c + 1) * P], xn[:, k, c * P:(c + 1) * P],
                                               ident[:])
                last.then_inc(moe[n].x_mm, 1)

            def routed(n):
                m = moe[n]

                base = n * TILES

                def step(it, k):
                    j, par = 4 * it + k, k % 2
                    if exists(j, 0, TILES - 2):
                        turn(n, (k + 1) % 4, it + (k + 1) // 4, 1 - par, j + 2)
                    if exists(j, 1, TILES):
                        pe.wait_ge(m.mul, j)
                        if isinstance(j, int) and j == 1:
                            pe.wait_ge(ffn[n].added, HALF * BEFORE)
                        wait(pe, tile_part.h_lo, base + j - 2)
                        nc.tensor.transpose(bank[4 + 1 - par][:, 0:P], ht[:], ident[:]).then_inc(m.h_mm, 1)
                    if exists(j, 0, TILES - 1):
                        pe.wait_ge(tile_part.x_lo, base + j + 1)
                        pe.wait_ge(tile_part.front_lo, base + j + 1)
                        wait(pe, m.mul, j - 1)
                        i = 0
                        for c in range(HC):
                            if c == 1:
                                last.then_inc(tile_part.front_mm, 1)
                                pe.wait_ge(tile_part.middle_lo, base + j + 1)
                            if c == 2:
                                pe.wait_ge(tile_part.back_lo, base + j + 1)
                            piece, start = (tfront, 0) if c == 0 else (tback[par], (c - 1) * FRONT)
                            for a, b in PARTS:
                                last = nc.tensor.matmul(bank[par][:, 0:2 * INTER], xT[par][a][:, c, :],
                                                        piece[b][:, start:start + FRONT],
                                                        start=(i == 0), stop=(i == 3 * HC - 1))
                                i += 1
                        last.then_inc(m.gu_mm, 1)
                    if exists(j, 1, TILES):
                        pe.wait_ge(tile_part.h_lo, base + j)
                        pe.wait_ge(tile_part.dn_lo, base + j)
                        wait(pe, m.y_out, j - 2)
                        for i, (a, b) in enumerate(PARTS):
                            last = nc.tensor.matmul(bank[6 + 1 - par][:], hT[a][:], tdn[1 - par][b][:],
                                                    start=(i == 0), stop=(i == 2))
                        last.then_inc(m.y_mm, 1)

                for k in range(4):
                    step(0, k)
                with pe.Fori(1, TILES // 4) as it:
                    for k in range(4):
                        step(it, k)
                for k in range(TILES % 4 + 1):
                    step(TILES // 4, k)
            def attention():
                def project(w, b, before, into=bank[0]):
                    wait(pe, att.proj_out, before)
                    m = 0
                    for c in range(HC):
                        for a, z in PARTS:
                            last = nc.tensor.matmul(into[:], w[a][:, c, :], xnT[z][:, c, b * SEQ:(b + 1) * SEQ],
                                                    start=(m == 0), stop=(m == 3 * HC - 1))
                            m += 1
                    last.then_inc(att.proj_mm, 1)

                def turn_value(before):
                    wait(pe, att.proj_out, before)
                    for j in range(ST):
                        last = nc.tensor.transpose(bank[0][:, j * P:(j + 1) * P], vT[:, j * P:(j + 1) * P], ident[:])
                    last.then_inc(att.proj_mm, 1)

                def turn(par, j, b, at):
                    for i in range(j, ST):
                        last = nc.tensor.transpose(bank[b][:, at + (i - j) * P:at + (i - j + 1) * P],
                                                   sp_[par][:, TRI[i] + j * P:TRI[i] + (j + 1) * P], ident[:])
                    return last

                def slot(g, k):
                    u, par, r, b = 8 * g + k, k % 2, k % 4, (k // 4) % 2
                    quad = 2 * g + k // 4
                    before = PROJ_AHEAD + 7 * quad
                    if exists(u, 0, UNITS - 1):
                        if isinstance(u, int) and u == 0:
                            pe.wait_ge(att.proj_out, PROJ_AHEAD - 1)
                        else:
                            pe.wait_ge(att.proj_out, before - 1 if r == 0 else before + qpos(u, r - 1) + 1)
                        for n, (bk, tiles) in enumerate(((3, ((3, 0),)), (4, ((2, 0), (0, 384))), (5, ((1, 0),)))):
                            wait(pe, att.masked, 4 * (u - 1) + (1, 3, 4)[n])
                            for i, c in tiles:
                                for m, (a, z) in enumerate(PARTS):
                                    last = nc.tensor.matmul(bank[bk][:, c:c + P * (i + 1)], qT[a][:, i * P:(i + 1) * P],
                                                            kT[b][z][:, 0:P * (i + 1)], start=(m == 0), stop=(m == 2))
                            last.then_inc(att.s_mm, 1)
                    if exists(u, 1, UNITS):
                        pe.wait_ge(att.normed, 4 * u)
                        wait(pe, att.t_lo, 3 * (u - 1))
                        turn(1 - par, 0, 6, 0).then_inc(att.t_mm, 1)
                        turn(1 - par, 1, 7, 0).then_inc(att.t_mm, 1)
                    if exists(u, 0, UNITS - 2):
                        if k == 7:
                            pe.wait_ge(att.w_lo, 6 + 10 * g + 7)
                        elif k < 3:
                            wait(pe, att.w_lo, 6 + 10 * (g - 1) + 8 + k)
                        project(wqs[(k + 1) % 4], ((k + 1) // 4) % 2, before + qpos(u, r))
                    if exists(u, 1, UNITS):
                        pe.wait_ge(att.t_lo, 3 * (u - 1) + 1)
                        turn(1 - par, 2, 6, 0)
                        turn(1 - par, 3, 6, 256).then_inc(att.t_mm, 1)
                    if exists(u, 5, UNITS + 4):
                        ob = (0, 1, 1, 1, 1, 0, 0, 0)[k % 8]
                        tile = (r - 1) % 4
                        if r == 1:
                            pe.wait_ge(att.pv_lo, u - 1)
                        wait(pe, att.added, UNITS - HALF if isinstance(u, int) and u > UNITS else u - 5)
                        m = 0
                        for h in range(G):
                            if k == 5:
                                pe.wait_ge(att.w_lo, 6 + 10 * g + (3 if exists(u, 0, UNITS - 9) else 1) + h)
                            for a, z in PARTS:
                                last = nc.tensor.matmul(o_bank(u)[:], oT[ob][h][a][:, tile * P:(tile + 1) * P],
                                                        wds[h][z][:], start=(m == 0), stop=(m == 3 * G - 1))
                                m += 1
                        last.then_inc(att.o_mm, 1)
                    if exists(u, 1, UNITS):
                        bu = ((k - 1) // 4) % 2
                        wait(pe, att.pv_lo, u - 1)
                        for j in range(ST):
                            if j != 3:
                                pe.wait_ge(att.t_lo, 3 * (u - 1) + j + 1)
                            for m, (a, z) in enumerate(PARTS):
                                last = nc.tensor.matmul(bank[1][:, j * P:SEQ], vv[bu][a][:, j, :],
                                                        pT[z][:, COL[j]:COL[j] + SEQ - j * P],
                                                        start=(j == 0 and m == 0), stop=(j == ST - 1 and m == 2),
                                                        skip_group_check=True)
                        last.then_inc(att.pv_mm, 1)
                    if isinstance(u, int) and u == 1:
                        pe.wait_ge(att.proj_out, before + QPOS[1] + 1)
                        turn_norm(1, 1)
                        pe.wait_ge(norm[1].lo, TT)
                    if r and exists(u, 0, UNITS - 5):
                        at = before + XPOS[r]
                        if r == 1:
                            if k == 5:
                                pe.wait_ge(att.w_lo, 6 + 10 * g + 2)
                            project(wks, 1 - b, at)
                        if r == 2:
                            project(wvs, 1 - b, at)
                        if r == 3:
                            turn_value(at)

                pe.wait_ge(norm[1].lo, HALF)
                pe.wait_ge(att.w_lo, 1)
                project(wks, 0, 0)
                pe.wait_ge(att.w_lo, 2)
                project(wvs, 0, 0, bank[3])
                pe.wait_ge(att.w_lo, 3)
                pe.wait_ge(ffn[0].added, HALF * SLOTS)
                project(wqs[0], 0, 0, bank[4])
                turn_value(2)
                att_slots(pe, slot)
                att_tail(slot)

            def feed_forward(n):
                turn_norm(2 * n, 0)
                gate_up(n, 0)
                turn_norm(2 * n, 1)
                router(n)
                gate_up(n, 1)
                down(n, 0)
                rank(n)
                for s in range(2, BEFORE):
                    gate_up(n, s)
                    down(n, s - 1)
                turn(n, 0, 0, 0, 1)
                down(n, BEFORE - 1)
                routed(n)
                for s in range(BEFORE, SLOTS):
                    gate_up(n, s)
                    if s == BEFORE + 1:
                        pe.wait_ge(moe[n].y_out, TILES)
                    if s > BEFORE:
                        down(n, s - 1)
                down(n, SLOTS - 1)

            feed_forward(0)
            turn_norm(1, 0)
            attention()
            feed_forward(1)


def _layout(np, q, w_qkv, w_dense, gate, w_gate_up, w_down, sh_gate_up, sh_down):
    gu = w_gate_up.reshape(NEXP, 2, INTER, HC, P).transpose(0, 4, 3, 1, 2).reshape(NEXP, P, GU)
    sgu = sh_gate_up.reshape(2, NSH, INTER, HC, P).transpose(1, 4, 3, 0, 2).reshape(NSH, P, GU)
    dn = w_down.transpose(0, 2, 1)
    sdn = sh_down.reshape(HID, NSH, INTER).transpose(1, 2, 0)
    ffn_w = np.concatenate([np.concatenate([gu, dn], 2), np.concatenate([sgu, sdn], 2)], 0)
    gate_w = gate.reshape(NEXP, HC, P).transpose(2, 1, 0)
    nq = KV * G * D
    wq = w_qkv[:nq].reshape(KV, G, D, HC, P).transpose(0, 4, 1, 3, 2)
    wkv = w_qkv[nq:].reshape(2, KV, D, HC, P).transpose(1, 4, 0, 3, 2)
    wd = w_dense.reshape(HID, KV, G, D).transpose(1, 3, 2, 0)
    return dict(x=q.reshape(TOK, HID), ffn_w=ffn_w, gate_w=gate_w, wq=wq, wkv=wkv, wd=wd)


def kernel(**inputs):
    import numpy as np
    import concourse.bacc as bacc
    from concourse.bass_utils import run_bass_kernel_spmd

    a = {n: np.asarray(v) for n, v in inputs.items()}
    laid = _layout(np, a["L0_attn_q"], a["L0_attn_w_qkv"], a["L0_attn_w_dense"], a["L0_ffn_gate_w"],
                   a["L0_ffn_w_gate_up"], a["L0_ffn_w_down"], a["L0_ffn_shared_w_gate_up"], a["L0_ffn_shared_w_down"])
    nc = bacc.Bacc("TRN2", target_bir_lowering=False, num_devices=1)
    arrays, args = {}, []
    for name, v in laid.items():
        arrays[f"in_{name}"] = np.ascontiguousarray(v)
        args.append(nc.dram_tensor(f"in_{name}", v.shape, mybir.dt.from_np(v.dtype), kind="ExternalInput").ap())
    out = nc.dram_tensor("out_x", (TOK, HID), F32, kind="ExternalOutput").ap()
    build(nc, *args, out)
    r = run_bass_kernel_spmd(nc, [arrays], core_ids=[0])
    return r.results[0]["out_x"].reshape(BATCH, SEQ, HID)
```
